# Optimizing a Trainium2 kernel written in Bass

```python
import numpy as np
import jax
import jax.numpy as jnp

def _softmax(x, axis=-1):
    return jax.nn.softmax(x, axis=axis)

def _gelu(x):
    return jax.nn.gelu(x, approximate=True)

def _silu(x):
    return jax.nn.silu(x)

def _sigmoid(x):
    return jax.nn.sigmoid(x)

def _layernorm(x, axis=-1, eps=1e-05):
    m = jnp.mean(x, axis=axis, keepdims=True)
    v = jnp.var(x, axis=axis, keepdims=True)
    return (x - m) / jnp.sqrt(v + eps)

def _scatter_add(tgt, idx, src, axis=0):
    return tgt.at[idx].add(src)

def _segment_sum(src, seg, n):
    return jax.ops.segment_sum(src, seg, n)
kernel_name = 'mk_adaln_attn_ffn_d1_seqx_r8_d1d307'

def setup_inputs(seed: int=0):
    np.random.seed(seed)
    _w = jnp.asarray

    def _rec_inputs():
        import jax
        import jax.numpy as jnp
        _rk = jax.random.key(seed)
        x = -0.000125 + 0.9999 * jax.random.normal(jax.random.fold_in(_rk, 1), (64, 32, 512), jnp.float32)
        _lenS = 32 - jax.random.randint(jax.random.fold_in(_rk, 7), (64,), 0, max(1, 32 // 4) + 1, jnp.int32)
        _lenS2 = 32 - jax.random.randint(jax.random.fold_in(_rk, 8), (64,), 0, max(1, 32 // 4) + 1, jnp.int32)
        cond_128 = 0.0061147 + 1.02565 * jax.random.normal(jax.random.fold_in(_rk, 11), (64, 128), jnp.float32)
        fside_S_0 = -0.022604 + 0.987366 * jax.random.normal(jax.random.fold_in(_rk, 12), (32,), jnp.float32)
        return (x, cond_128, fside_S_0)
    x, cond_128, fside_S_0 = _rec_inputs()

    def _L0_cond_setup():
        import jax, jax.numpy as jnp
        import numpy as np
        K = 8
        T = 1.0
        D_EMBD = 128
        IN_C = 32
        OUT_C = 32
        BS = 32
        H = 512
        HID = 128
        key = jax.random.key(seed)
        ks = jax.random.split(key, 10)
        s = lambda fan_in: 1.0 / np.sqrt(fan_in)
        return {'x': jax.random.normal(ks[0], (BS, IN_C, H), dtype=jnp.float32), 'embedding': jax.random.normal(ks[1], (BS, D_EMBD), dtype=jnp.float32), 'W0': jax.random.normal(ks[2], (D_EMBD, HID), dtype=jnp.float32) * s(D_EMBD), 'b0': jnp.zeros((HID,), dtype=jnp.float32), 'W1': jax.random.normal(ks[3], (HID, HID), dtype=jnp.float32) * s(HID), 'b1': jnp.zeros((HID,), dtype=jnp.float32), 'W2': jax.random.normal(ks[4], (HID, K), dtype=jnp.float32) * s(HID), 'b2': jnp.zeros((K,), dtype=jnp.float32), 'weight': jax.random.normal(ks[5], (K, OUT_C, IN_C, 1), dtype=jnp.float32) * s(IN_C), 'bias_k': jax.random.normal(ks[6], (K, OUT_C), dtype=jnp.float32) * 0.1}
    _L0_cond_all = _L0_cond_setup()
    _L0_cond_in = {k: v for k, v in _L0_cond_all.items() if k in ('W0', 'b0', 'W1', 'b1', 'W2', 'b2', 'weight', 'bias_k')}
    del _L0_cond_all

    def _L0_attn_setup():
        import jax, jax.numpy as jnp
        import numpy as np
        B, T, D = (1, 256, 512)
        H, G = (32, 8)
        HD = D // H
        REP = H // G
        KV_DIM = 2 * HD * G
        key = jax.random.key(seed)
        k0, k1, k2, k3 = jax.random.split(key, 4)
        x = jax.random.normal(k0, (B, T, D), dtype=jnp.float32)
        Wq = jax.random.normal(k1, (D, D), dtype=jnp.float32) * 0.02
        Wkv = jax.random.normal(k2, (D, KV_DIM), dtype=jnp.float32) * 0.02
        Wo = jax.random.normal(k3, (D, D), dtype=jnp.float32) * 0.02
        bo = jnp.zeros((D,), dtype=jnp.float32)
        return {'x': x, 'Wq': Wq, 'Wkv': Wkv, 'Wo': Wo, 'bo': bo}
    _L0_attn_all = _L0_attn_setup()
    _L0_attn_in = {k: v for k, v in _L0_attn_all.items() if k in ('Wq', 'Wkv', 'Wo', 'bo')}
    del _L0_attn_all

    def _L0_cond2_setup():
        import jax, jax.numpy as jnp
        import numpy as np
        from jax import lax
        N, C_IN, L = (32, 32, 512)
        C_OUT, K, GROUPS = (32, 9, 4)
        C_DIM, PAD, STRIDE = (128, 4, 1)
        key = jax.random.key(seed)
        k1, k2, k3, k4, k5 = jax.random.split(key, 5)
        x = jax.random.normal(k1, (N, C_IN, L), dtype=jnp.float32)
        c = jax.random.normal(k2, (N, C_DIM), dtype=jnp.float32)
        weight = jax.random.normal(k3, (C_OUT, C_IN // GROUPS, K), dtype=jnp.float32)
        c_weight = jax.random.normal(k4, (C_OUT, C_DIM), dtype=jnp.float32)
        bias = jax.random.normal(k5, (C_OUT,), dtype=jnp.float32)
        return {'x': x, 'c': c, 'weight': weight, 'c_weight': c_weight, 'bias': bias}
    _L0_cond2_all = _L0_cond2_setup()
    _L0_cond2_in = {k: v for k, v in _L0_cond2_all.items() if k in ('weight', 'c_weight')}
    del _L0_cond2_all

    def _L0_ffn_setup():
        import jax, jax.numpy as jnp
        import numpy as np
        DIM = 512
        HID = 1376
        R = 16
        SCALING = 32.0 / 16.0

        def _lora_linear(x, w, a, b):
            base = jnp.einsum('bsd,od->bso', x, w)
            low = jnp.einsum('bsr,or->bso', jnp.einsum('bsd,rd->bsr', x, a), b)
            return base + low * SCALING
        key = jax.random.key(seed)
        ks = jax.random.split(key, 10)
        s_in = 1.0 / np.sqrt(DIM)
        s_hid = 1.0 / np.sqrt(HID)
        return {'x': jax.random.normal(ks[0], (4, 256, DIM), jnp.float32), 'w1': jax.random.normal(ks[1], (HID, DIM), jnp.float32) * s_in, 'w3': jax.random.normal(ks[2], (HID, DIM), jnp.float32) * s_in, 'w2': jax.random.normal(ks[3], (DIM, HID), jnp.float32) * s_hid, 'lora_A1': jax.random.normal(ks[4], (R, DIM), jnp.float32) * s_in, 'lora_B1': jax.random.normal(ks[5], (HID, R), jnp.float32) * 0.02, 'lora_A3': jax.random.normal(ks[6], (R, DIM), jnp.float32) * s_in, 'lora_B3': jax.random.normal(ks[7], (HID, R), jnp.float32) * 0.02, 'lora_A2': jax.random.normal(ks[8], (R, HID), jnp.float32) * s_hid, 'lora_B2': jax.random.normal(ks[9], (DIM, R), jnp.float32) * 0.02}
    _L0_ffn_all = _L0_ffn_setup()
    _L0_ffn_in = {k: v for k, v in _L0_ffn_all.items() if k in ('w1', 'w3', 'w2', 'lora_A1', 'lora_B1', 'lora_A3', 'lora_B3', 'lora_A2', 'lora_B2')}
    del _L0_ffn_all
    return {'x': x, 'cond_128': cond_128, 'fside_S_0': fside_S_0, 'L0_cond_W0': _L0_cond_in['W0'], 'L0_cond_b0': _L0_cond_in['b0'], 'L0_cond_W1': _L0_cond_in['W1'], 'L0_cond_b1': _L0_cond_in['b1'], 'L0_cond_W2': _L0_cond_in['W2'], 'L0_cond_b2': _L0_cond_in['b2'], 'L0_cond_weight': _L0_cond_in['weight'], 'L0_cond_bias_k': _L0_cond_in['bias_k'], 'L0_attn_Wq': _L0_attn_in['Wq'], 'L0_attn_Wkv': _L0_attn_in['Wkv'], 'L0_attn_Wo': _L0_attn_in['Wo'], 'L0_attn_bo': _L0_attn_in['bo'], 'L0_cond2_weight': _L0_cond2_in['weight'], 'L0_cond2_c_weight': _L0_cond2_in['c_weight'], 'L0_ffn_w1': _L0_ffn_in['w1'], 'L0_ffn_w3': _L0_ffn_in['w3'], 'L0_ffn_w2': _L0_ffn_in['w2'], 'L0_ffn_lora_A1': _L0_ffn_in['lora_A1'], 'L0_ffn_lora_B1': _L0_ffn_in['lora_B1'], 'L0_ffn_lora_A3': _L0_ffn_in['lora_A3'], 'L0_ffn_lora_B3': _L0_ffn_in['lora_B3'], 'L0_ffn_lora_A2': _L0_ffn_in['lora_A2'], 'L0_ffn_lora_B2': _L0_ffn_in['lora_B2']}

def reference(x, cond_128, fside_S_0, L0_cond_W0, L0_cond_b0, L0_cond_W1, L0_cond_b1, L0_cond_W2, L0_cond_b2, L0_cond_weight, L0_cond_bias_k, L0_attn_Wq, L0_attn_Wkv, L0_attn_Wo, L0_attn_bo, L0_cond2_weight, L0_cond2_c_weight, L0_ffn_w1, L0_ffn_w3, L0_ffn_w2, L0_ffn_lora_A1, L0_ffn_lora_B1, L0_ffn_lora_A3, L0_ffn_lora_B3, L0_ffn_lora_A2, L0_ffn_lora_B2):
    import jax
    import jax.numpy as jnp

    def _L0_cond_ref(x, embedding, W0, b0, W1, b1, W2, b2, weight, bias_k):
        import jax, jax.numpy as jnp
        import numpy as np
        K = 8
        T = 1.0
        D_EMBD = 128
        IN_C = 32
        OUT_C = 32
        BS = 32
        H = 512
        HID = 128
        h = jax.nn.gelu(embedding @ W0 + b0, approximate=False)
        h = jax.nn.gelu(h @ W1 + b1, approximate=False)
        att = jax.nn.softmax((h @ W2 + b2) / T, axis=-1)
        agg_w = jnp.einsum('bk,koi->boi', att, weight[..., 0])
        agg_b = att @ bias_k
        out = jnp.einsum('boi,bih->boh', agg_w, x) + agg_b[:, :, None]
        return out

    def _L0_attn_ref(x, Wq, Wkv, Wo, bo):
        import jax, jax.numpy as jnp
        import numpy as np
        B, T, D = (1, 256, 512)
        H, G = (32, 8)
        HD = D // H
        REP = H // G
        KV_DIM = 2 * HD * G
        b, t, d = x.shape
        q = jnp.dot(x, Wq).reshape(b, t, H, HD).transpose(0, 2, 1, 3)
        kv = jnp.dot(x, Wkv).reshape(b, t, G, 2, HD).transpose(2, 3, 0, 1, 4)
        k, v = (kv[:, 0], kv[:, 1])
        k = jnp.broadcast_to(k[:, :, None], (G, b, REP, t, HD)).reshape(b, H, t, HD)
        v = jnp.broadcast_to(v[:, :, None], (G, b, REP, t, HD)).reshape(b, H, t, HD)
        scores = jnp.einsum('bhqd,bhkd->bhqk', q, k)
        causal = jnp.triu(jnp.ones((t, t), dtype=bool), 1)
        scores = jnp.where(causal[None, None], -jnp.inf, scores)
        weights = jax.nn.softmax(scores * (1.0 / HD ** 0.5), axis=-1)
        ctx = jnp.einsum('bhqk,bhkd->bhqd', weights, v)
        ctx = ctx.transpose(0, 2, 1, 3).reshape(b, t, d)
        return jnp.dot(ctx, Wo) + bo

    def _L0_cond2_ref(x, c, weight, c_weight, bias):
        import jax, jax.numpy as jnp
        import numpy as np
        from jax import lax
        N, C_IN, L = (32, 32, 512)
        C_OUT, K, GROUPS = (32, 9, 4)
        C_DIM, PAD, STRIDE = (128, 4, 1)
        out = lax.conv_general_dilated(x, weight, window_strides=(STRIDE,), padding=[(PAD, PAD)], dimension_numbers=('NCH', 'OIH', 'NCH'), feature_group_count=GROUPS)
        ctx = jnp.einsum('nd,od->no', c, c_weight)
        out = out + ctx[:, :, None] + bias[None, :, None]
        return out

    def _L0_ffn_ref(x, w1, w3, w2, lora_A1, lora_B1, lora_A3, lora_B3, lora_A2, lora_B2):
        import jax, jax.numpy as jnp
        import numpy as np
        DIM = 512
        HID = 1376
        R = 16
        SCALING = 32.0 / 16.0

        def _lora_linear(x, w, a, b):
            base = jnp.einsum('bsd,od->bso', x, w)
            low = jnp.einsum('bsr,or->bso', jnp.einsum('bsd,rd->bsr', x, a), b)
            return base + low * SCALING
        h1 = _lora_linear(x, w1, lora_A1, lora_B1)
        h3 = _lora_linear(x, w3, lora_A3, lora_B3)
        g = jax.nn.silu(h1) * h3
        return _lora_linear(g, w2, lora_A2, lora_B2)
    x = x + _L0_attn_ref(_L0_cond_ref(x, cond_128, L0_cond_W0, L0_cond_b0, L0_cond_W1, L0_cond_b1, L0_cond_W2, L0_cond_b2, L0_cond_weight, L0_cond_bias_k), L0_attn_Wq, L0_attn_Wkv, L0_attn_Wo, L0_attn_bo)
    x = x + _L0_ffn_ref(_L0_cond2_ref(x, cond_128, L0_cond2_weight, L0_cond2_c_weight, fside_S_0), L0_ffn_w1, L0_ffn_w3, L0_ffn_w2, L0_ffn_lora_A1, L0_ffn_lora_B1, L0_ffn_lora_A3, L0_ffn_lora_B3, L0_ffn_lora_A2, L0_ffn_lora_B2)
    return x

_drawn_inputs = setup_inputs


def setup_inputs(seed=0):
    import zlib

    import numpy as np

    out = dict(_drawn_inputs(seed))
    spreads = {'L0_cond_b0': (0.0, 0.8),
     'L0_cond_b1': (0.0, 2.0),
     'L0_cond_b2': (0.0, 2.0),
     'L0_attn_bo': (0.0, 0.528)}
    factors = {'L0_cond_W0': 8.0,
     'L0_cond_W1': 8.0,
     'L0_cond_W2': 8.0,
     'L0_cond_weight': 3.131,
     'L0_cond_bias_k': 8.0,
     'L0_attn_Wq': 8.0,
     'L0_attn_Wkv': 3.504,
     'L0_attn_Wo': 3.505,
     'fside_S_0': 3.423}
    for name, (base, spread) in spreads.items():
        noise = np.random.default_rng([zlib.crc32(name.encode()), seed]).standard_normal(out[name].shape)
        drawn = base * np.exp(spread * noise) if base else spread * noise
        out[name] = jnp.asarray(drawn.astype(out[name].dtype))
    for name, factor in factors.items():
        out[name] = (out[name] * factor).astype(out[name].dtype)
    return out
```

```python
from contextlib import ExitStack

import numpy as np

import concourse.bass as bass
from concourse import mybir

F32 = mybir.dt.float32
ALU = mybir.AluOpType
ACT = mybir.ActivationFunctionType
AX_X = mybir.AxisListType.X

P = 128
B, S, D = 64, 32, 512
N = B * S
COND = 128
K = 8
G, REP, HD = 8, 4, 16
GD = G * HD
TAPS, CG = 9, 8
HID, R = 1376, 16
LORA_SCALE = 2.0
BLOCK = 512
BLOCKS = N // BLOCK
TILES = BLOCK // P
BB = BLOCK // S
BT = P // S
PAIRS = BB // 2
DC = D // P
HC = -(-HID // P)
HW = [min(P, HID - h * P) for h in range(HC)]
NEAR = 3
SCALE = HD ** -0.5
FOLD_N = HID // 4
QG = B // G
HALF = BB // 2
USES = DC + 1 + REP + 1
PROJECTED = USES * BLOCKS
PROBS = 4
TURN = 3
CONTEXT = TURN + 1
OUT = CONTEXT + 2


def adaln_attention_ffn(nc, x, cond_t, w0, b0, w1, b1, w2, b2, mix_w, mix_b, wq, wk, wv, wo, bo,
                        conv, conv_cond, conv_bias, f1, f3, f2, a1, a3, a2, lb1, lb3, lb2,
                        ident, causal, out):
    with ExitStack() as ctx:
        def sb(name, shape, stage=ctx):
            return stage.enter_context(nc.sbuf_tensor(name, shape, F32))

        def sem(name):
            return ctx.enter_context(nc.semaphore(name))

        cond_sb = sb("cond_sb", [COND, B])
        w0_sb = sb("w0_sb", [COND, COND])
        w1_sb = sb("w1_sb", [COND, COND])
        w2_sb = sb("w2_sb", [COND, K])
        b0_sb = sb("b0_sb", [COND, 1])
        b1_sb = sb("b1_sb", [COND, 1])
        b2_sb = sb("b2_sb", [1, K])
        mixb_sb = sb("mixb_sb", [K, S])
        convc_sb = sb("convc_sb", [COND, S])
        convb_sb = sb("convb_sb", [1, S])
        bo_sb = sb("bo_sb", [1, D])
        ident_sb = sb("ident_sb", [P, P])
        causal_sb = sb("causal_sb", [P, S])
        ones = sb("ones", [P, P])
        wq_sb = sb("wq_sb", [P, DC, REP, GD])
        wk_sb = sb("wk_sb", [P, DC, GD])
        wv_sb = sb("wv_sb", [P, DC, GD])
        wo_sb = sb("wo_sb", [GD, REP, D])
        f3_sb = sb("f3_sb", [P, DC, HID])
        hid0 = sb("hid0", [COND, B])
        hid1 = sb("hid1", [COND, B])
        neg_top = sb("neg_top", [B, 1])
        att = sb("att", [B, K])
        att_sum = sb("att_sum", [B, 1])
        att_inv = sb("att_inv", [B, 1])
        att_t = sb("att_t", [K, B])
        convb_row = sb("convb_row", [1, BB, S])
        convb_all = sb("convb_all", [P, N])
        bo_all = sb("bo_all", [P, D])

        ps = [ctx.enter_context(nc.psum_tensor(f"ps{n}", [P, 512], F32)) for n in range(8)]

        cond_loaded = sem("cond_loaded")
        attn_loaded = sem("attn_loaded")
        f3_loaded = sem("f3_loaded")
        up_loaded = sem("up_loaded")
        down_loaded = sem("down_loaded")
        x_loaded = [sem("x_loaded"), sem("x_loaded_in_rows")]
        ones_set = sem("ones_set")
        zeros_set = sem("zeros_set")
        cond_pe = sem("cond_pe")
        cond_act = sem("cond_act")
        cond_dve = sem("cond_dve")
        mix_made = sem("mix_made")
        spread_pe = sem("spread_pe")
        spread_act = sem("spread_act")
        terms_made = sem("terms_made")
        front_filled = sem("front_filled")
        front_emptied = [sem("front0_emptied"), sem("front1_emptied")]
        v_cleared = sem("v_cleared")
        q_loaded = [sem(f"q_half{n}_loaded") for n in range(2)]
        k_loaded = [sem(f"k_half{n}_loaded") for n in range(2)]
        v_spread = sem("v_spread")
        scores_ready = sem("scores_ready")
        masked = sem("masked")
        top_ready = sem("top_ready")
        shifted = sem("shifted")
        exp_ready = sem("exp_ready")
        sum_ready = sem("sum_ready")
        inv_ready = sem("inv_ready")
        probs_ready = sem("probs_ready")
        turned = sem("turned")
        turned_copied = sem("turned_copied")
        ctx_filled = sem("ctx_filled")
        ctx_copied = sem("ctx_copied")
        x_reloaded = sem("x_reloaded")
        resid_ready = sem("resid_ready")
        x1_stored = [sem(f"x1_tile{t}_stored") for t in range(TILES)]
        fold_filled = sem("fold_filled")
        folded = sem("folded")
        near_zeroed = sem("near_zeroed")
        near_loaded = sem("near_loaded")
        x1_loaded = sem("x1_loaded")
        conv_filled = sem("conv_filled")
        conv_copied = sem("conv_copied")
        up1_filled = sem("up1_filled")
        up3_filled = sem("up3_filled")
        silu_ready = sem("silu_ready")
        gate_ready = sem("gate_ready")
        down_filled = sem("down_filled")
        out_ready = sem("out_ready")
        out_stored = sem("out_stored")

        x1_dram = nc.dram_tensor("x1_dram", [N, D], F32).ap()

        x_sb = sb("x_sb", [P, TILES, D])
        rows = sb("rows", [P, TILES, D])
        ctx_t = sb("ctx_t", [GD, REP, BLOCK])
        top = sb("top", [P, PROBS, 2 * G])
        total = sb("total", [P, PROBS, 2 * G])
        inv = sb("inv", [P, PROBS, 2 * G])
        with ExitStack() as room:
            mix = sb("mix", [P, N // P, BT, S], room)
            mixb_all = sb("mixb_all", [P, N], room)
        with ExitStack() as room:
            near = sb("near", [P, BB, P + 2], room)
        sb("room0", [P, 2 * N])
        with ExitStack() as room:
            y_t = [sb(f"y{n}_t", [P, DC, BLOCK], room) for n in range(2)]
        with ExitStack() as room:
            v_wide = sb("v_wide", [P, BB, 2, G, HD], room)
        sb("room1", [P, 2 * DC * BLOCK])
        with ExitStack() as room:
            mixw_sb = sb("mixw_sb", [K, S, BT, S], room)
            mixb_terms = sb("mixb_terms", [K, B, S], room)
            convb_terms = sb("convb_terms", [COND, B, S], room)
        with ExitStack() as room:
            q_all = sb("q_all", [GD, B, REP, S], room)
        with ExitStack() as room:
            f1_sb = sb("f1_sb", [P, DC, HID], room)
            a13_sb = sb("a13_sb", [S + R, D], room)
            lb13_sb = sb("lb13_sb", [S + R, HID], room)
            conv_sb = sb("conv_sb", [P, NEAR, P], room)
        sb("room2", [P, B * REP * S])
        with ExitStack() as room:
            q_t = sb("q_t", [GD, BB, REP, S], room)
            k_all = sb("k_all", [GD, G, QG, S], room)
            v_all = sb("v_all", [P, N // P, GD], room)
            k_wide = sb("k_wide", [GD, 2, G, QG, S], room)
        with ExitStack() as room:
            f2_sb = sb("f2_sb", [P, HC, D], room)
            a2_sb = sb("a2_sb", [R, HID], room)
            lb2_sb = sb("lb2_sb", [R, D], room)
            silu = sb("silu", [P, 2, BLOCK], room)
        sb("room3", [P, 5 * BB * REP * S])
        with ExitStack() as room:
            probs = sb("probs", [P, PROBS, 2, G, S], room)
            probs_t = sb("probs_t", [P, 2, 4, P], room)
        with ExitStack() as room:
            c_t = sb("c_t", [P, DC, BLOCK], room)
            gate = sb("gate", [P, 2, BLOCK], room)
        sb("room4", [P, 6 * BLOCK])

        front = ps[0:2]
        score_bank = ps[2:4]
        turn_bank = ps[4:6]
        ctx_bank = ps[6:8]
        up_bank = ps[0:4]
        down_bank = ps[4:8]

        x_rows = x.rearrange("(t p) d -> p t d", p=P)
        x1_rows = x1_dram.rearrange("(t p) d -> p t d", p=P)
        out_rows = out.rearrange("(t p) d -> p t d", p=P)
        x1_near = x1_dram.rearrange("(b s) (r n) -> r s b n", s=S, r=BT)

        cond_loads = [(cond_sb[:, :], cond_t), (w0_sb[:, :], w0), (b0_sb[:, :], b0), (w1_sb[:, :], w1),
                      (b1_sb[:, :], b1), (w2_sb[:, :], w2), (b2_sb[:, :], b2), (ident_sb[:, :], ident),
                      (mixb_sb[:, :], mix_b), (convc_sb[:, :], conv_cond), (convb_sb[:, :], conv_bias),
                      (bo_sb[:, :], bo)] + [(mixw_sb[:, :, c, :], mix_w) for c in range(BT)]
        attn_loads = [(wk_sb[:, :, :], wk), (wq_sb[:, :, :, :], wq), (wv_sb[:, :, :], wv),
                      (causal_sb[:, :], causal), (wo_sb[:, :, :], wo)]
        up_loads = [(a13_sb[0:R, :], a1), (lb13_sb[0:R, :], lb1), (a13_sb[S:S + R, :], a3),
                    (lb13_sb[S:S + R, :], lb3), (f1_sb[:, :, :], f1), (conv_sb[:, :, :], conv)]
        down_loads = [(a2_sb[:, :], a2), (lb2_sb[:, :], lb2),
                      (f2_sb[:, 0:HC - 1, :], f2[0:(HC - 1) * P, :].rearrange("(c p) d -> p c d", p=P)),
                      (f2_sb[0:HW[-1], HC - 1, :], f2[(HC - 1) * P:HID, :])]

        up_folds, down_folds = [], []
        for f, first in ((f1_sb, 0), (f3_sb, S)):
            a, lb = a13_sb[first:first + R, :], lb13_sb[first:first + R, :]
            for c in range(DC):
                for n in range(HID // FOLD_N):
                    cols = slice(n * FOLD_N, (n + 1) * FOLD_N)
                    up_folds.append((f[:, c, cols], a[:, c * P:(c + 1) * P], lb[:, cols]))
        for h, w in enumerate(HW):
            down_folds.append((f2_sb[0:w, h, :], a2_sb[:, h * P:h * P + w], lb2_sb[:, :]))
        folds = up_folds + down_folds
        conv_order = [2, 3, 0, 1]

        def pipeline(eng, step):
            for s in range(PAIRS):
                step(0, s, True, True)
            with eng.Fori(1, BLOCKS) as i:
                for s in range(PAIRS):
                    step(i, s, True, False)
            for s in range(PAIRS, PAIRS + OUT - 1):
                step(BLOCKS - 1, s, False, False)

        def emptied(use):
            return use // 2 + 1

        def blocks(eng, body):
            body(0, True, True)
            with eng.Fori(1, BLOCKS - 1) as i:
                body(i, False, True)
            body(BLOCKS - 1, False, False)

        block = ctx.enter_context(nc.Block())

        @block.sync
        def _(sp):
            for dst, src in cond_loads:
                sp.dma_start(dst, src).then_inc(cond_loaded, 16)
            sp.dma_start(f3_sb[:, :, :], f3).then_inc(f3_loaded, 16)
            for i in range(2, BLOCKS):
                sp.wait_ge(front_filled, (i - 2) * USES + DC)
                sp.dma_start((x_sb, rows)[i % 2][:, :, :], x_rows[:, i * TILES:(i + 1) * TILES, :])\
                    .then_inc(x_loaded[i % 2], 16)

            def queries_and_keys(g):
                i, half = g // 2, g % 2
                if g >= 2:
                    sp.wait_ge(scores_ready, (i - 1) * PAIRS + (half + 1) * PAIRS // 2)
                sp.dma_start(q_t[:, half * HALF:(half + 1) * HALF, :, :],
                             q_all[:, g * HALF:(g + 1) * HALF, :, :]).then_inc(q_loaded[half], 16)
                for k in range(G):
                    sp.dma_start(k_wide[k * HD:(k + 1) * HD, half, k, :, :],
                                 k_all[g * HD:(g + 1) * HD, k, :, :]).then_inc(k_loaded[half], 16)

            def store_x1(i, t):
                sp.wait_ge(front_emptied[t % 2], emptied(PROJECTED + i * TILES + t) + 1)
                sp.dma_start(x1_rows[:, i * TILES + t, :], rows[:, t, :]).then_inc(x1_stored[t], 16)

            sp.wait_ge(front_emptied[0], emptied(PROJECTED))
            sp.wait_ge(front_emptied[1], emptied(PROJECTED))
            sp.wait_ge(zeros_set, 2)
            for g in range(2):
                queries_and_keys(g)
            sp.dma_start(x_sb[:, :, :], x_rows[:, 0:TILES, :]).then_inc(x_reloaded, 16)
            for i in range(BLOCKS):
                if i + 1 < BLOCKS:
                    queries_and_keys(2 * i + 2)
                    store_x1(i, 0)
                    queries_and_keys(2 * i + 3)
                    sp.wait_ge(resid_ready, (i + 1) * TILES)
                    sp.dma_start(x_sb[:, :, :], x_rows[:, (i + 1) * TILES:(i + 2) * TILES, :])\
                        .then_inc(x_reloaded, 16)
                else:
                    sp.wait_ge(q_loaded[0], 16 * BLOCKS)
                    sp.wait_ge(q_loaded[1], 16 * BLOCKS)
                    for dst, src in up_loads:
                        sp.dma_start(dst, src).then_inc(up_loaded, 16)
                    store_x1(i, 0)
                    sp.wait_ge(scores_ready, BLOCKS * PAIRS)
                    for dst, src in down_loads:
                        sp.dma_start(dst, src).then_inc(down_loaded, 16)
                for t in range(1, TILES):
                    store_x1(i, t)

            def load_near(i):
                for r in range(BT):
                    sp.dma_start(near[r * S:(r + 1) * S, :, 1:P + 1],
                                 x1_near[r, :, bass.ds(i * BB, BB), :]).then_inc(near_loaded, 16)

            def load_rows(i):
                sp.dma_start(rows[:, :, :], x1_rows[:, bass.ds(i * TILES, TILES), :]).then_inc(x1_loaded, 16)

            def store_out(i):
                for t in range(TILES):
                    sp.wait_ge(out_ready, i * TILES + t + 1)
                    sp.dma_start(out_rows[:, bass.ds(i * TILES + t, 1), :],
                                 rows[:, t:t + 1, :]).then_inc(out_stored, 16)

            for stored in x1_stored:
                sp.wait_ge(stored, 16 * BLOCKS)
            load_near(0)
            load_rows(0)
            with sp.Fori(0, BLOCKS - 1) as i:
                sp.wait_ge(conv_filled, (i + 1) * BT)
                load_near(i + 1)
                store_out(i)
                sp.wait_ge(out_stored, (i + 1) * TILES * 16)
                load_rows(i + 1)
            store_out(BLOCKS - 1)
            sp.wait_ge(out_stored, 16 * TILES * BLOCKS)

        @block.gpsimd
        def _(pool):
            pool.memset(ones[:, :], 1.0).then_inc(ones_set, 1)
            pool.memset(mix[:, :, :, :], 0.0).then_inc(zeros_set, 1)
            pool.wait_ge(cond_loaded, 16 * len(cond_loads))
            pool.tensor_tensor(convb_terms[:, :, :], cond_sb[:, :].unsqueeze(2).to_broadcast([COND, B, S]),
                               convc_sb[:, :].unsqueeze(1).to_broadcast([COND, B, S]), ALU.mult)\
                .then_inc(terms_made, 1)
            pool.memset(k_wide[:, :, :, :, :], 0.0).then_inc(zeros_set, 1)
            pool.wait_ge(front_filled, PROJECTED)
            pool.memset(v_wide[:, :, :, :, :], 0.0).then_inc(v_cleared, 1)
            pool.wait_ge(spread_act, 9)

            def step(i, s, start, first):
                n = i * PAIRS + s
                if start:
                    pool.wait_ge(top_ready, n + 1)
                    pr = probs[:, s % PROBS].rearrange("p b g k -> p (b g) k")
                    pool.tensor_tensor(pr, pr, top[:, s % PROBS].unsqueeze(2).to_broadcast([P, 2 * G, S]),
                                       ALU.subtract).then_inc(shifted, 1)
                if (s >= 1 or not first) and s < PAIRS + 1:
                    pool.wait_ge(inv_ready, n)
                    pr = probs[:, (s - 1) % PROBS].rearrange("p b g k -> p (b g) k")
                    pool.tensor_tensor(pr, pr, inv[:, (s - 1) % PROBS].unsqueeze(2).to_broadcast([P, 2 * G, S]),
                                       ALU.mult).then_inc(probs_ready, 1)
                if start and s % 2:
                    t = s // 2
                    if t == 0:
                        pool.wait_ge(x_reloaded, (i + 1) * 16)
                    if not first:
                        pool.wait_ge(x1_stored[t], i * 16)
                    pool.tensor_tensor(rows[:, t, :].rearrange("p (r n) -> p r n", r=BT),
                                       x_sb[:, t, :].rearrange("p (n r) -> p r n", r=BT),
                                       bo_all[:, :].rearrange("p (r n) -> p r n", r=BT), ALU.add)\
                        .then_inc(resid_ready, 1)

            pipeline(pool, step)
            pool.memset(near[:, :, 0:1], 0.0).then_inc(near_zeroed, 1)
            pool.memset(near[:, :, P + 1:P + 2], 0.0).then_inc(near_zeroed, 1)

        @block.scalar
        def _(act):
            act.dma_start(x_sb[:, :, :], x_rows[:, 0:TILES, :]).then_inc(x_loaded[0], 16)
            act.dma_start(rows[:, :, :], x_rows[:, TILES:2 * TILES, :]).then_inc(x_loaded[1], 16)
            for dst, src in attn_loads:
                act.dma_start(dst, src).then_inc(attn_loaded, 16)
            act.wait_ge(cond_loaded, 16 * len(cond_loads))
            act.wait_ge(cond_pe, 1)
            act.activation(hid0[:, :], ps[0][:, 0:B], ACT.Gelu, bias=b0_sb[:, 0:1]).then_inc(cond_act, 1)
            act.wait_ge(cond_pe, 2)
            act.activation(hid1[:, :], ps[1][:, 0:B], ACT.Gelu, bias=b1_sb[:, 0:1]).then_inc(cond_act, 1)
            act.wait_ge(cond_dve, 1)
            act.activation(att[:, :], ps[2][0:B, 0:K], ACT.Exp, bias=neg_top[:, 0:1],
                           accum_out=att_sum[:, 0:1]).then_inc(cond_act, 1)
            for n in range(9):
                act.wait_ge(spread_pe, n + 1)
                dst = (mixb_all[:, n * 512:(n + 1) * 512] if n < 4 else
                       convb_all[:, (n - 4) * 512:(n - 3) * 512] if n < 8 else bo_all[:, :])
                act.copy(dst, ps[4 + n % 2][:, :]).then_inc(spread_act, 1)
            with act.Fori(0, BLOCKS // 2) as i:
                for half in range(2):
                    use = (2 * i + half) * USES
                    n = DC
                    act.wait_ge(front_filled, use + n + 1)
                    act.copy(k_all[:, :, bass.ds((2 * i + half) * 2, 2), :].rearrange("p g c s -> p c g s"),
                             front[n % 2][:, :].rearrange("p (c g s) -> p c g s", c=2, s=S))\
                        .then_inc(front_emptied[n % 2], 1)
                    for j in range(REP):
                        n = DC + 1 + j
                        act.wait_ge(front_filled, use + n + 1)
                        act.copy(q_all[:, bass.ds((2 * i + half) * BB, BB), j, :],
                                 front[n % 2][:, :].rearrange("p (b s) -> p b s", s=S))\
                            .then_inc(front_emptied[n % 2], 1)
                    n = DC + 1 + REP
                    act.wait_ge(front_filled, use + n + 1)
                    act.copy(v_all[:, bass.ds((2 * i + half) * TILES, TILES), :],
                             front[n % 2][:, :].rearrange("p (t c) -> p t c", t=TILES))\
                        .then_inc(front_emptied[n % 2], 1)

            def step(i, s, start, first):
                n = i * PAIRS + s
                if start:
                    act.wait_ge(shifted, n + 1)
                    act.activation(probs[:, s % PROBS], probs[:, s % PROBS], ACT.Exp, scale=SCALE)\
                        .then_inc(exp_ready, 1)
                if (s >= TURN or not first) and s - TURN < PAIRS:
                    act.wait_ge(turned, n - TURN + 1)
                    act.copy(probs_t[:, (s - TURN) % 2], turn_bank[(s - TURN) % 2][:, :]
                             .rearrange("p (c q) -> p c q", q=P)).then_inc(turned_copied, 1)
                if (s >= CONTEXT or not first) and s - CONTEXT < PAIRS:
                    q = (s - CONTEXT) % PAIRS
                    act.wait_ge(ctx_filled, n - CONTEXT + 1)
                    act.copy(ctx_t[:, :, q * 2 * S:(q + 1) * 2 * S].rearrange("p j (b s) -> p b j s", s=S),
                             ctx_bank[q % 2][:, 0:2 * P].rearrange("p (b j s) -> p b j s", b=2, j=REP))\
                        .then_inc(ctx_copied, 1)

            pipeline(act, step)

            def block_of_rows(i, first, more):
                for h, w in enumerate(HW):
                    act.wait_ge(up1_filled, i * HC + h + 1)
                    if h >= 2 or not first:
                        act.wait_ge(gate_ready, i * HC + max(h - 1, 0))
                    act.activation(silu[0:w, h % 2, :], up_bank[2 * (h % 2)][0:w, :], ACT.Silu)\
                        .then_inc(silu_ready, 1)

            blocks(act, block_of_rows)

        @block.vector
        def _(dve):
            dve.wait_ge(cond_pe, 3)
            dve.tensor_reduce(neg_top[:, :], ps[2][0:B, 0:K], AX_X, ALU.max, negate=True).then_inc(cond_dve, 1)
            dve.wait_ge(cond_act, 3)
            dve.reciprocal(att_inv[:, :], att_sum[:, :]).then_inc(cond_dve, 1)
            dve.wait_ge(cond_dve, 2)
            dve.tensor_scalar(att[:, :], att[:, :], att_inv[:, 0:1], None, ALU.mult).then_inc(cond_dve, 1)
            dve.wait_ge(cond_pe, 4)
            dve.tensor_copy(att_t[:, :], ps[3][0:K, 0:B]).then_inc(cond_dve, 1)
            dve.tensor_copy(convb_row[:, :, :], convb_sb[:, :].unsqueeze(1).to_broadcast([1, BB, S]))\
                .then_inc(terms_made, 1)
            dve.wait_ge(cond_dve, 4)
            dve.tensor_tensor(mixb_terms[:, :, :], att_t[:, :].unsqueeze(2).to_broadcast([K, B, S]),
                              mixb_sb[:, :].unsqueeze(1).to_broadcast([K, B, S]), ALU.mult)\
                .then_inc(terms_made, 1)
            dve.wait_ge(zeros_set, 1)
            for n in range(4):
                dve.wait_ge(cond_pe, 5 + n)
                made = ps[n][:, :].rearrange("p (o t c) -> p t o c", o=8, c=BT)
                for c in range(BT):
                    copy = dve.tensor_copy(mix[c * S:(c + 1) * S, :, c, n * 8:(n + 1) * 8],
                                           made[c * S:(c + 1) * S, :, :, c])
                copy.then_inc(front_emptied[n] if n < 2 else mix_made, 1)
            dve.wait_ge(spread_act, 9)
            with dve.Fori(0, BLOCKS // 2) as i:
                for half in range(2):
                    for c in range(DC):
                        dve.wait_ge(front_filled, (2 * i + half) * USES + c + 1)
                        dve.tensor_tensor(y_t[half][:, c, :], front[c % 2][:, :],
                                          mixb_all[:, bass.ds((2 * i + half) * BLOCK, BLOCK)], ALU.add)\
                            .then_inc(front_emptied[c % 2], 1)
            dve.wait_ge(attn_loaded, 16 * len(attn_loads))
            dve.wait_ge(front_emptied[1], emptied(PROJECTED))
            dve.wait_ge(v_cleared, 1)

            def spread_values(i, half):
                vg = v_all[:, :, :].rearrange("p (c h) (g d) -> p c h g d", h=2, d=HD)
                vw = v_wide[:, half * HALF:(half + 1) * HALF, :, :, :].rearrange("p c h (z g) d -> p c h z g d", z=2)
                for g in range(BT):
                    for h in range(2):
                        dve.tensor_copy(vw[g * S:(g + 1) * S, :, h, h, g, :],
                                        vg[g * S:(g + 1) * S, :, h, bass.ds(2 * i + half, 1), :]
                                        .rearrange("p c g d -> p c (g d)")).then_inc(v_spread, 1)

            def step(i, s, start, first):
                n = i * PAIRS + s
                if start:
                    pr = probs[:, s % PROBS].rearrange("p b g k -> p (b g) k")
                    dve.wait_ge(scores_ready, n + 1)
                    if s >= PROBS or not first:
                        dve.wait_ge(turned, n - PROBS + 1)
                    dve.tensor_tensor(pr, score_bank[s % 2][:, :].rearrange("p (c k) -> p c k", k=S),
                                      causal_sb[:, :].unsqueeze(1).to_broadcast([P, 2 * G, S]), ALU.add)\
                        .then_inc(masked, 1)
                    dve.wait_ge(masked, n + 1)
                    dve.tensor_reduce(top[:, s % PROBS, :], pr, AX_X, ALU.max).then_inc(top_ready, 1)
                if (s >= 1 or not first) and s < PAIRS + 1:
                    q = (s - 1) % PROBS
                    dve.wait_ge(exp_ready, n)
                    dve.tensor_reduce(total[:, q, :], probs[:, q].rearrange("p b g k -> p (b g) k"),
                                      AX_X, ALU.add).then_inc(sum_ready, 1)
                    dve.wait_ge(sum_ready, n)
                    dve.reciprocal(inv[:, q, :], total[:, q, :]).then_inc(inv_ready, 1)
                if start and s == 0:
                    if not first:
                        dve.wait_ge(ctx_filled, i * PAIRS - PAIRS // 2)
                    spread_values(i, 0)
                if start and s == CONTEXT:
                    if not first:
                        dve.wait_ge(ctx_filled, i * PAIRS)
                    spread_values(i, 1)
                if s % 2 == 0 and (s >= OUT or not first):
                    t = (s - OUT) // 2 % TILES
                    tile = i * TILES + (s - OUT) // 2
                    dve.wait_ge(front_filled, PROJECTED + tile + 1)
                    dve.wait_ge(resid_ready, tile + 1)
                    dve.tensor_tensor(rows[:, t, :], front[t % 2][:, :], rows[:, t, :], ALU.add)\
                        .then_inc(front_emptied[t % 2], 1)

            pipeline(dve, step)

            def fold(n):
                dst = folds[n][0]
                dve.wait_ge(fold_filled, n + 1)
                dve.scalar_tensor_tensor(out=dst, in0=up_bank[n % 4][0:dst.shape[0], 0:dst.shape[1]],
                                         scalar=LORA_SCALE, in1=dst, op0=ALU.mult, op1=ALU.add)\
                    .then_inc(folded, 1)

            def copy_conv(i):
                for n, q in enumerate(conv_order):
                    dve.wait_ge(conv_filled, i * BT + n + 1)
                    cb = convb_all[:, bass.ds(i * BLOCK + q * P, P)].rearrange("p (b o) -> p b o", o=S)
                    dve.tensor_tensor(c_t[:, :, q * P:(q + 1) * P].rearrange("p s (b o) -> p b s o", o=S),
                                      up_bank[q][:, :].rearrange("p (b s o) -> p b s o", s=DC, o=S),
                                      cb.unsqueeze(2).to_broadcast([P, BT, DC, S]), ALU.add)\
                        .then_inc(conv_copied, 1)

            def block_of_rows(i, first, more):
                for h, w in enumerate(HW):
                    dve.wait_ge(up3_filled, i * HC + h + 1)
                    dve.wait_ge(silu_ready, i * HC + h + 1)
                    dve.tensor_tensor(gate[0:w, h % 2, :], up_bank[2 * (h % 2) + 1][0:w, :], silu[0:w, h % 2, :],
                                      ALU.mult).then_inc(gate_ready, 1)
                if more:
                    copy_conv(i + 1)
                dve.wait_ge(x1_loaded, 16 * (i + 1))
                for t in range(TILES):
                    dve.wait_ge(down_filled, i * TILES + t + 1)
                    dve.tensor_tensor(rows[:, t, :], down_bank[t][:, :], rows[:, t, :], ALU.add)\
                        .then_inc(out_ready, 1)

            for n in range(len(up_folds)):
                fold(n)
            copy_conv(0)
            for n in range(len(up_folds), len(folds)):
                fold(n)
            blocks(dve, block_of_rows)

        @block.tensor
        def _(pe):
            pe.wait_ge(cond_loaded, 16 * len(cond_loads))
            pe.matmul(ps[0][:, 0:B], w0_sb[:, :], cond_sb[:, :], start=True, stop=True).then_inc(cond_pe, 1)
            pe.wait_ge(cond_act, 1)
            pe.matmul(ps[1][:, 0:B], w1_sb[:, :], hid0[:, :], start=True, stop=True).then_inc(cond_pe, 1)
            pe.wait_ge(ones_set, 1)
            pe.wait_ge(cond_act, 2)
            pe.matmul(ps[2][0:B, 0:K], hid1[:, :], w2_sb[:, :], start=True, stop=False)
            pe.matmul(ps[2][0:B, 0:K], ones[0:1, 0:B], b2_sb[:, :], start=False, stop=True).then_inc(cond_pe, 1)
            pe.wait_ge(cond_dve, 3)
            pe.transpose(ps[3][0:K, 0:B], att[:, :], ident_sb[0:B, 0:B]).then_inc(cond_pe, 1)
            pe.wait_ge(cond_dve, 4)
            for o in range(S):
                mm = pe.matmul(ps[o // 8][:, (o % 8) * B:(o % 8 + 1) * B],
                               mixw_sb[:, o, :, :].rearrange("k c i -> k (c i)"), att_t[:, :],
                               start=True, stop=True)
                if o % 8 == 7:
                    mm.then_inc(cond_pe, 1)
            pe.wait_ge(terms_made, 3)
            for n in range(9):
                if n >= 2:
                    pe.wait_ge(spread_act, n - 1)
                bank = ps[4 + n % 2][:, :]
                if n < 4:
                    rhs = mixb_terms[:, n * BB:(n + 1) * BB, :].rearrange("k b o -> k (b o)")
                    pe.matmul(bank, ones[0:K, :], rhs, start=True, stop=True).then_inc(spread_pe, 1)
                elif n < 8:
                    rhs = convb_terms[:, (n - 4) * BB:(n - 3) * BB, :].rearrange("k b o -> k (b o)")
                    pe.matmul(bank, ones[:, :], rhs, start=True, stop=False)
                    pe.matmul(bank, ones[0:1, :], convb_row[:, :, :].rearrange("k b o -> k (b o)"),
                              start=False, stop=True).then_inc(spread_pe, 1)
                else:
                    pe.matmul(bank, ones[0:1, :], bo_sb[:, :], start=True, stop=True).then_inc(spread_pe, 1)
            pe.wait_ge(front_emptied[0], emptied(0))
            pe.wait_ge(front_emptied[1], emptied(1))
            pe.wait_ge(mix_made, 2)
            pe.wait_ge(attn_loaded, 16 * len(attn_loads))
            pe.wait_ge(spread_act, 9)
            with pe.Fori(0, BLOCKS // 2) as i:
                for half, buf in enumerate((x_sb, rows)):
                    blk = 2 * i + half

                    def bank_free(n):
                        pe.wait_ge(front_emptied[n % 2], blk * (USES // 2) + emptied(n))

                    pe.wait_ge(x_loaded[half], 16 * (i + 1))
                    for c in range(DC):
                        bank_free(c)
                        for t in range(TILES):
                            mm = pe.matmul(front[c % 2][:, t * P:(t + 1) * P], buf[:, t, c * P:(c + 1) * P],
                                           mix[:, bass.ds(blk * TILES + t, 1), :, :]
                                           .rearrange("p t c o -> p (t c o)"), start=True, stop=True)
                        mm.then_inc(front_filled, 1)
                    bank_free(DC + 1)
                    for n in range(DC, DC + 1 + REP):
                        bank_free(n)
                        for c in range(DC):
                            w = wk_sb[:, c, :] if n == DC else wq_sb[:, c, n - DC - 1, :]
                            mm = pe.matmul(front[n % 2][:, :], w, y_t[half][:, c, :],
                                           start=(c == 0), stop=(c == DC - 1))
                        mm.then_inc(front_filled, 1)
                    n = DC + 1 + REP
                    bank_free(n)
                    for t in range(TILES):
                        for c in range(DC):
                            mm = pe.matmul(front[n % 2][:, t * P:(t + 1) * P], y_t[half][:, c, t * P:(t + 1) * P],
                                           wv_sb[:, c, :], start=(c == 0), stop=(c == DC - 1))
                    mm.then_inc(front_filled, 1)

            def step(i, s, start, first):
                n = i * PAIRS + s
                if start:
                    if s % (PAIRS // 2) == 0:
                        half = s // (PAIRS // 2)
                        pe.wait_ge(q_loaded[half], (i + 1) * 16)
                        pe.wait_ge(k_loaded[half], (i + 1) * G * 16)
                    if s >= 2 or not first:
                        pe.wait_ge(masked, n - 1)
                    for b in range(2):
                        c = 2 * s + b
                        mm = pe.matmul(score_bank[s % 2][:, b * G * S:(b + 1) * G * S],
                                       q_t[:, c, :, :].rearrange("p j s -> p (j s)"),
                                       k_wide[:, c // HALF, :, c % HALF, :], start=True, stop=True)
                    mm.then_inc(scores_ready, 1)
                if (s >= TURN or not first) and s - TURN < PAIRS:
                    q = s - TURN
                    pe.wait_ge(probs_ready, n - TURN + 1)
                    if q >= 2 or not first:
                        pe.wait_ge(turned_copied, n - TURN - 1)
                    for b in range(2):
                        for h in range(2):
                            mm = pe.transpose(turn_bank[q % 2][:, (2 * b + h) * P:(2 * b + h + 1) * P],
                                              probs[:, q % PROBS, b, 4 * h:4 * h + 4, :].rearrange("p g k -> p (g k)"),
                                              ident_sb[:, :])
                    mm.then_inc(turned, 1)
                if (s >= CONTEXT or not first) and s - CONTEXT < PAIRS:
                    q = (s - CONTEXT) % PAIRS
                    if q % (PAIRS // 2) == 0:
                        half = (s - CONTEXT) // (PAIRS // 2)
                        pe.wait_ge(v_spread, (2 * i + half + 1) * 2 * BT)
                    pe.wait_ge(turned_copied, n - CONTEXT + 1)
                    if s - CONTEXT >= 2 or not first:
                        pe.wait_ge(ctx_copied, n - CONTEXT - 1)
                    for b in range(2):
                        for h in range(2):
                            mm = pe.matmul(ctx_bank[q % 2][:, b * P:(b + 1) * P],
                                           v_wide[:, 2 * q + b, h].rearrange("p g d -> p (g d)"),
                                           probs_t[:, q % 2, 2 * b + h, :], start=(h == 0), stop=(h == 1))
                    mm.then_inc(ctx_filled, 1)
                if s % 2 == 0 and (s >= OUT or not first):
                    t = (s - OUT) // 2 % TILES
                    tile = i * TILES + (s - OUT) // 2
                    pe.wait_ge(ctx_copied, n - OUT + 2)
                    pe.wait_ge(front_emptied[t % 2], emptied(PROJECTED) + i * (TILES // 2) + (s - OUT) // 2 // 2)
                    for j in range(REP):
                        mm = pe.matmul(front[t % 2][:, :], ctx_t[:, j, t * P:(t + 1) * P], wo_sb[:, j, :],
                                       start=(j == 0), stop=(j == REP - 1))
                    mm.then_inc(front_filled, 1)

            pipeline(pe, step)

            def fold(n):
                dst, a, lb = folds[n]
                if n >= 4:
                    pe.wait_ge(folded, n - 3)
                pe.matmul(up_bank[n % 4][0:dst.shape[0], 0:dst.shape[1]], a, lb, start=True, stop=True)\
                    .then_inc(fold_filled, 1)

            def convolve(i, first=False):
                pe.wait_ge(near_loaded, 16 * BT * (i + 1))
                for q in conv_order:
                    if not first:
                        pe.wait_ge(gate_ready, i * HC - (1 if q >= 2 else 0))
                    for b in range(BT):
                        for m in range(NEAR):
                            mm = pe.matmul(up_bank[q][:, b * P:(b + 1) * P], near[:, q * BT + b, m:m + P],
                                           conv_sb[:, m, :], start=(m == 0), stop=(m == NEAR - 1))
                    mm.then_inc(conv_filled, 1)

            def up(i, h):
                if h >= 2:
                    pe.wait_ge(gate_ready, i * HC + h - 1)
                for f, bank, filled in ((f1_sb, up_bank[2 * (h % 2)], up1_filled),
                                        (f3_sb, up_bank[2 * (h % 2) + 1], up3_filled)):
                    for c in range(DC):
                        mm = pe.matmul(bank[0:HW[h], :], f[:, c, h * P:h * P + HW[h]], c_t[:, c, :],
                                       start=(c == 0), stop=(c == DC - 1))
                    mm.then_inc(filled, 1)

            def down(i, h, first):
                pe.wait_ge(gate_ready, i * HC + h + 1)
                if h == 0 and not first:
                    pe.wait_ge(out_ready, i * TILES)
                for t in range(TILES):
                    mm = pe.matmul(down_bank[t][:, :], gate[0:HW[h], h % 2, t * P:(t + 1) * P],
                                   f2_sb[0:HW[h], h, :], start=(h == 0), stop=(h == HC - 1))
                    if h == HC - 1:
                        mm.then_inc(down_filled, 1)

            def block_of_rows(i, first, more):
                pe.wait_ge(conv_copied, BT * (i + 1))
                up(i, 0)
                for h in range(1, HC - 1):
                    up(i, h)
                    down(i, h - 1, first)
                up(i, HC - 1)
                if more:
                    convolve(i + 1)
                down(i, HC - 2, first)
                down(i, HC - 1, first)

            pe.wait_ge(up_loaded, 16 * len(up_loads))
            pe.wait_ge(f3_loaded, 16)
            pe.wait_ge(front_emptied[0], emptied(PROJECTED + BLOCKS * TILES))
            pe.wait_ge(front_emptied[1], emptied(PROJECTED + BLOCKS * TILES))
            for n in range(len(up_folds)):
                fold(n)
            pe.wait_ge(near_zeroed, 2)
            pe.wait_ge(folded, len(up_folds))
            convolve(0, first=True)
            pe.wait_ge(down_loaded, 16 * len(down_loads))
            pe.wait_ge(conv_copied, BT)
            for n in range(len(up_folds), len(folds)):
                fold(n)
            pe.wait_ge(folded, len(folds))
            blocks(pe, block_of_rows)


def layouts(a):
    perm = lambda w: w.reshape(*w.shape[:-1], P, BT).swapaxes(-1, -2).reshape(w.shape)
    wkv = a["L0_attn_Wkv"].reshape(DC, P, G, 2, HD)
    conv = np.zeros((BT, S, NEAR, BT, S), a["L0_cond2_weight"].dtype)
    for m in range(NEAR):
        for r in range(BT):
            for s in range(BT):
                tap = BT * (m - 1) + r - s + TAPS // 2
                if 0 <= tap < TAPS:
                    for co in range(S):
                        first = co // CG * CG
                        conv[r, first:first + CG, m, s, co] = a["L0_cond2_weight"][co, :, tap]
    t = lambda w: w.swapaxes(-1, -2)
    return {
        "x": a["x"].reshape(N, D), "cond_t": t(a["cond_128"]),
        "w0": a["L0_cond_W0"], "b0": a["L0_cond_b0"].reshape(COND, 1),
        "w1": a["L0_cond_W1"], "b1": a["L0_cond_b1"].reshape(COND, 1),
        "w2": a["L0_cond_W2"], "b2": a["L0_cond_b2"].reshape(1, K),
        "mix_w": a["L0_cond_weight"].reshape(K, S, S), "mix_b": a["L0_cond_bias_k"],
        "wq": a["L0_attn_Wq"].reshape(DC, P, G, REP, HD).transpose(1, 0, 3, 2, 4).reshape(P, DC, REP, GD),
        "wk": wkv[:, :, :, 0].transpose(1, 0, 2, 3).reshape(P, DC, GD),
        "wv": wkv[:, :, :, 1].transpose(1, 0, 2, 3).reshape(P, DC, GD),
        "wo": perm(a["L0_attn_Wo"].reshape(G, REP, HD, D).transpose(0, 2, 1, 3)).reshape(GD, REP, D),
        "bo": perm(a["L0_attn_bo"].reshape(1, D)),
        "conv": conv.reshape(P, NEAR, P), "conv_cond": t(a["L0_cond2_c_weight"]),
        "conv_bias": a["fside_S_0"].reshape(1, S),
        "f1": a["L0_ffn_w1"].reshape(HID, P, BT).transpose(1, 2, 0),
        "f3": a["L0_ffn_w3"].reshape(HID, P, BT).transpose(1, 2, 0),
        "f2": perm(t(a["L0_ffn_w2"])),
        "a1": perm(a["L0_ffn_lora_A1"]), "a3": perm(a["L0_ffn_lora_A3"]), "a2": a["L0_ffn_lora_A2"],
        "lb1": t(a["L0_ffn_lora_B1"]), "lb3": t(a["L0_ffn_lora_B3"]), "lb2": perm(t(a["L0_ffn_lora_B2"])),
        "ident": np.eye(P, dtype=np.float32),
        "causal": np.where(np.arange(S)[None, :] > np.arange(P)[:, None] % S, -1e30, 0.0).astype(np.float32),
    }


def kernel(**inputs):
    import concourse.bacc as bacc
    from concourse.bass_utils import run_bass_kernel_spmd

    nc = bacc.Bacc("TRN2", target_bir_lowering=False, num_devices=1)
    arrays = {f"in_{k}": np.ascontiguousarray(v) for k, v in
              layouts({k: np.asarray(v) for k, v in inputs.items()}).items()}
    args = {k[3:]: nc.dram_tensor(k, v.shape, mybir.dt.from_np(v.dtype), kind="ExternalInput").ap()
            for k, v in arrays.items()}
    out = nc.dram_tensor("out", (N, D), F32, kind="ExternalOutput").ap()
    adaln_attention_ffn(nc, out=out, **args)
    r = run_bass_kernel_spmd(nc, [arrays], core_ids=[0])
    got = r.results[0]["out"]
    return got.reshape(B, S, BT, P).swapaxes(2, 3).reshape(B, S, D)
```

```python
from contextlib import ExitStack

import numpy as np

import concourse.bass as bass
from concourse import mybir

F32 = mybir.dt.float32
F32R = mybir.dt.float32r
ALU = mybir.AluOpType
ACT = mybir.ActivationFunctionType
AX_X = mybir.AxisListType.X

P = 128
B, S, D = 64, 32, 512
N = B * S
COND = 128
K = 8
G, REP, HD = 8, 4, 16
GD = G * HD
TAPS, CG = 9, 8
HID, R = 1376, 16
LORA_SCALE = 2.0
BLOCK = 512
BLOCKS = N // BLOCK
TILES = BLOCK // P
BB = BLOCK // S
BT = P // S
PAIRS = BB // 2
DC = D // P
HC = -(-HID // P)
HW = [min(P, HID - h * P) for h in range(HC)]
NEAR = 3
SCALE = HD ** -0.5
FOLD_N = HID // BLOCKS
PARTS = 7
STACK = 3 * S
QG = B // G
HALF = BB // 2
USES = DC + 1 + REP + 1
PROJECTED = USES * BLOCKS
PROBS = 4
TURN = 3
CONTEXT = TURN + 1
OUT = CONTEXT + 2
FOLDS = 2 * DC * BLOCKS
SPLITS = 3 * HC
F2_HEAD = 8


def adaln_attention_ffn(nc, x, cond_t, w0, b0, w1, b1, w2, b2, mix_w, mix_b, wq, wk, wv, wo, bo,
                        conv, conv_cond, conv_bias, f1, f3, f2, a1, a3, a2, lb1, lb3, lb2,
                        ident, causal, out):
    with ExitStack() as ctx:
        def sb(name, shape, stage=ctx, dtype=F32):
            return stage.enter_context(nc.sbuf_tensor(name, shape, dtype))

        def sem(name):
            return ctx.enter_context(nc.semaphore(name))

        cond_sb = sb("cond_sb", [COND, B])
        w0_sb = sb("w0_sb", [COND, COND])
        w1_sb = sb("w1_sb", [COND, COND])
        w2_sb = sb("w2_sb", [COND, K])
        b0_sb = sb("b0_sb", [COND, 1])
        b1_sb = sb("b1_sb", [COND, 1])
        b2_sb = sb("b2_sb", [1, K])
        mixb_sb = sb("mixb_sb", [K, S])
        convc_sb = sb("convc_sb", [COND, S])
        convb_sb = sb("convb_sb", [1, S])
        ident_sb = sb("ident_sb", [P, P])
        causal_sb = sb("causal_sb", [P, S])
        ones = sb("ones", [P, P])
        conv_sb = sb("conv_sb", [P, NEAR, P])
        hid0 = sb("hid0", [COND, B])
        hid1 = sb("hid1", [COND, B])
        neg_top = sb("neg_top", [B, 1])
        att = sb("att", [B, K])
        att_sum = sb("att_sum", [B, 1])
        att_inv = sb("att_inv", [B, 1])
        att_t = sb("att_t", [K, B])
        convb_all = sb("convb_all", [P, N])
        bo_all = sb("bo_all", [P, D])

        ps = [ctx.enter_context(nc.psum_tensor(f"ps{n}", [P, 512], F32)) for n in range(8)]

        cond_loaded = sem("cond_loaded")
        attn_loaded = sem("attn_loaded")
        ffn_loaded = sem("ffn_loaded")
        f2_loaded = sem("f2_loaded")
        x_loaded = [sem("x_loaded"), sem("x_loaded_in_rows")]
        ones_set = sem("ones_set")
        zeros_set = sem("zeros_set")
        cond_pe = sem("cond_pe")
        cond_act = sem("cond_act")
        cond_dve = sem("cond_dve")
        mix_made = sem("mix_made")
        spread_pe = sem("spread_pe")
        spread_act = sem("spread_act")
        terms_made = sem("terms_made")
        front_filled = sem("front_filled")
        front_emptied = [sem("front0_emptied"), sem("front1_emptied")]
        v_cleared = sem("v_cleared")
        q_stored = [sem(f"q_block{n}_stored") for n in range(2)]
        up_factors_cleared = sem("up_factors_cleared")
        up_factors_loaded = sem("up_factors_loaded")
        up_stacked = sem("up_stacked")
        down_factors_cleared = sem("down_factors_cleared")
        down_factors_loaded = sem("down_factors_loaded")
        down_stacked = sem("down_stacked")
        up_folded = sem("up_folded")
        hi_split = sem("hi_split")
        lo_split = sem("lo_split")
        c_ready = sem("c_ready")
        c_hi_ready = sem("c_hi_ready")
        c_lo_ready = sem("c_lo_ready")
        gate_hi_ready = sem("gate_hi_ready")
        gate_lo_ready = sem("gate_lo_ready")
        q_loaded = [sem(f"q_half{n}_loaded") for n in range(2)]
        k_loaded = [sem(f"k_half{n}_loaded") for n in range(2)]
        v_spread = sem("v_spread")
        scores_ready = sem("scores_ready")
        masked = sem("masked")
        top_ready = sem("top_ready")
        shifted = sem("shifted")
        exp_ready = sem("exp_ready")
        sum_ready = sem("sum_ready")
        inv_ready = sem("inv_ready")
        probs_ready = sem("probs_ready")
        turned = sem("turned")
        turned_copied = sem("turned_copied")
        ctx_filled = sem("ctx_filled")
        ctx_copied = sem("ctx_copied")
        x_reloaded = sem("x_reloaded")
        resid_ready = sem("resid_ready")
        x1_stored = [sem(f"x1_tile{t}_stored") for t in range(TILES)]
        up_fold_filled = sem("up_fold_filled")
        down_fold_filled = sem("down_fold_filled")
        down_folded = sem("down_folded")
        near_zeroed = sem("near_zeroed")
        near_loaded = sem("near_loaded")
        x1_loaded = sem("x1_loaded")
        conv_filled = sem("conv_filled")
        up1_filled = sem("up1_filled")
        up3_filled = sem("up3_filled")
        silu_ready = sem("silu_ready")
        gate_ready = sem("gate_ready")
        down_filled = sem("down_filled")
        out_ready = sem("out_ready")
        out_stored = sem("out_stored")

        x1_dram = nc.dram_tensor("x1_dram", [N, D], F32).ap()
        q_dram = nc.dram_tensor("q_dram", [GD, B, REP, S], F32).ap()

        rows = sb("rows", [P, TILES, D])
        top = sb("top", [P, PROBS, 2 * G])
        total = sb("total", [P, PROBS, 2 * G])
        inv = sb("inv", [P, PROBS, 2 * G])
        with ExitStack() as room:
            mix = sb("mix", [P, N // P, BT, S], room)
            mixb_all = sb("mixb_all", [P, N], room)
            wk_sb = sb("wk_sb", [P, DC, GD], room)
            wv_sb = sb("wv_sb", [P, DC, GD], room)
        with ExitStack() as room:
            sb("room0_head", [P, HC * DC * P - 2 * HID - D], room)
            a_down = sb("a_down", [STACK, HID], room)
            b_down = sb("b_down", [STACK, D], room)
        with ExitStack() as room:
            sb("room0_head_again", [P, HC * DC * P - 2 * HID - D], room)
            a_down_s = sb("a_down_s", [STACK, HID], room, F32R)
            b_down_s = sb("b_down_s", [STACK, D], room, F32R)
            down_part = sb("down_part", [STACK, HID], room, F32R)
        with ExitStack() as room:
            f3_hi = sb("f3_hi", [P, HC, DC, P], room, F32R)
        sb("room0", [P, HC * DC * P])
        with ExitStack() as room:
            y_t = [sb(f"y{n}_t", [P, DC, BLOCK], room) for n in range(2)]
        with ExitStack() as room:
            v_wide = sb("v_wide", [P, BB, 2, G, HD], room)
        with ExitStack() as room:
            c_hi = sb("c_hi", [P, DC, BLOCK], room, F32R)
            c_lo = sb("c_lo", [P, DC, BLOCK], room, F32R)
        sb("room1", [P, 2 * DC * BLOCK])
        with ExitStack() as room:
            k_all = sb("k_all", [GD, G, QG, S], room)
            v_all = sb("v_all", [P, N // P, GD], room)
            wq_sb = sb("wq_sb", [P, DC, REP, GD], room)
        with ExitStack() as room:
            f2_sb = sb("f2_sb", [P, HC, D], room)
        with ExitStack() as room:
            f2_lo = sb("f2_lo", [P, HC, D], room, F32R)
            c_odd = sb("c_odd", [P, BT, DC, S], room)
        sb("room2", [P, 3 * N])
        with ExitStack() as room:
            k_wide = sb("k_wide", [GD, 2, G, QG, S], room)
            q_t = sb("q_t", [GD, BB, REP, S], room)
        with ExitStack() as room:
            f2_hi_head = sb("f2_hi_head", [P, F2_HEAD, D], room, F32R)
            near = sb("near", [P, BB, P + 2], room)
        sb("room3", [P, F2_HEAD * D + BB * (P + 2)])
        with ExitStack() as room:
            convb_row = sb("convb_row", [1, BB, S], room)
            bo_sb = sb("bo_sb", [1, D], room)
        with ExitStack() as room:
            probs = sb("probs", [P, PROBS, 2, G, S], room)
            probs_t = sb("probs_t", [P, 2, 4, P], room)
        with ExitStack() as room:
            gate_hi = sb("gate_hi", [P, 2, BLOCK], room, F32R)
            gate_lo = sb("gate_lo", [P, 2, BLOCK], room, F32R)
            gate = sb("gate", [P, 2, BLOCK], room)
        sb("room4", [P, 6 * BLOCK])
        with ExitStack() as room:
            q_odd = sb("q_odd", [GD, BB, REP, S], room)
        with ExitStack() as room:
            ctx_t = sb("ctx_t", [GD, REP, BLOCK], room)
        with ExitStack() as room:
            f2_hi_tail = sb("f2_hi_tail", [P, HC - F2_HEAD, D], room, F32R)
            c_even = sb("c_even", [P, BT, DC, S], room)
        sb("room5", [P, REP * BLOCK])
        with ExitStack() as room:
            mixw_sb = sb("mixw_sb", [K, S, BT, S], room)
            mixb_terms = sb("mixb_terms", [K, B, S], room)
            convb_terms = sb("convb_terms", [COND, B, S], room)
        with ExitStack() as room:
            f1_sb = sb("f1_sb", [P, DC, HID], room)
            a_up = sb("a_up", [STACK, 2, D], room)
            b_up = sb("b_up", [STACK, HID], room)
        with ExitStack() as room:
            f1_lo = sb("f1_lo", [P, DC, HID], room, F32R)
            a_up_s = sb("a_up_s", [STACK, 2, D], room, F32R)
            b_up_s = sb("b_up_s", [STACK, HID], room, F32R)
        sb("room6", [P, 4 * N])
        with ExitStack() as room:
            f3_sb = sb("f3_sb", [P, DC, HID], room)
        with ExitStack() as room:
            f3_lo = sb("f3_lo", [P, DC, HID], room, F32R)
        sb("room7", [P, DC * HID])
        with ExitStack() as room:
            x_sb = sb("x_sb", [P, TILES, D], room)
            wo_sb = sb("wo_sb", [GD, REP, D], room)
            up_part = sb("up_part", [STACK, HID], room, F32R)
        with ExitStack() as room:
            f1_hi = sb("f1_hi", [P, DC, HID], room, F32R)
        sb("room8", [P, DC * HID])
        c_raw = (c_even, c_odd)
        a_up_rows = a_up[:, :, :].rearrange("k f d -> k (f d)")
        a_up_s_rows = a_up_s[:, :, :].rearrange("k f d -> k (f d)")
        q_stage = (q_t, q_odd)

        front = ps[0:2]
        score_bank = ps[2:4]
        turn_bank = ps[4:6]
        ctx_bank = ps[6:8]
        up_bank = ps[0:4]
        down_bank = ps[4:8]
        fold_bank = ps[4:8]

        x_rows = x.rearrange("(t p) d -> p t d", p=P)
        x1_rows = x1_dram.rearrange("(t p) d -> p t d", p=P)
        out_rows = out.rearrange("(t p) d -> p t d", p=P)
        x1_near = x1_dram.rearrange("(b s) (r n) -> r s b n", s=S, r=BT)

        cond_loads = [(cond_sb[:, :], cond_t), (w0_sb[:, :], w0), (b0_sb[:, :], b0), (w1_sb[:, :], w1),
                      (b1_sb[:, :], b1), (w2_sb[:, :], w2), (b2_sb[:, :], b2), (ident_sb[:, :], ident),
                      (mixb_sb[:, :], mix_b), (convc_sb[:, :], conv_cond), (convb_sb[:, :], conv_bias),
                      (bo_sb[:, :], bo)] + [(mixw_sb[:, :, c, :], mix_w) for c in range(BT)]
        attn_loads = [(wk_sb[:, :, :], wk), (wq_sb[:, :, :, :], wq), (wv_sb[:, :, :], wv),
                      (causal_sb[:, :], causal), (wo_sb[:, :, :], wo)]
        up_factor_loads = []
        for n in range(3):
            for f, (a, lb) in enumerate(((a1, lb1), (a3, lb3))):
                rank = slice(n * S + f * R, n * S + (f + 1) * R)
                up_factor_loads += [(a_up[rank, f, :], a), (b_up[rank, :], lb)]
        down_factor_loads = []
        for n in range(3):
            rank = slice(n * S, n * S + R)
            down_factor_loads += [(a_down[rank, :], a2), (b_down[rank, :], lb2)]
        f2_loads = [(f2_sb[:, 0:HC - 1, :], f2[0:(HC - 1) * P, :].rearrange("(c p) d -> p c d", p=P)),
                    (f2_sb[0:HW[-1], HC - 1, :], f2[(HC - 1) * P:HID, :])]

        def f2_hi(h):
            return (f2_hi_head[0:HW[h], h, :] if h < F2_HEAD else f2_hi_tail[0:HW[h], h - F2_HEAD, :])

        def split_parts(h):
            w, cols = HW[h], slice(h * P, h * P + HW[h])
            return ((f3_sb[:, :, cols], f3_hi[:, h, :, 0:w], f3_lo[:, :, cols]),
                    (f1_sb[:, :, cols], f1_hi[:, :, cols], f1_lo[:, :, cols]),
                    (f2_sb[0:w, h, :], f2_hi(h), f2_lo[0:w, h, :]))

        up_folds = [(f3_sb, c, 1) for c in range(DC)] + [(f1_sb, c, 0) for c in range(DC)]
        conv_order = [2, 3, 0, 1]

        def pipeline(eng, step):
            for s in range(PAIRS):
                step(0, s, True, True)
            with eng.Fori(1, BLOCKS) as i:
                for s in range(PAIRS):
                    step(i, s, True, False)
            for s in range(PAIRS, PAIRS + OUT - 1):
                step(BLOCKS - 1, s, False, False)

        def emptied(use):
            return use // 2 + 1

        def blocks(eng, body):
            body(0, True, True)
            with eng.Fori(1, BLOCKS - 1) as i:
                body(i, False, True)
            body(BLOCKS - 1, False, False)

        block = ctx.enter_context(nc.Block())

        @block.sync
        def _(sp):
            for dst, src in cond_loads:
                sp.dma_start(dst, src).then_inc(cond_loaded, 16)
            sp.dma_start(f3_sb[:, :, :], f3).then_inc(ffn_loaded, 16)
            sp.wait_ge(up_factors_cleared, 2)
            for dst, src in up_factor_loads:
                sp.dma_start(dst, src).then_inc(up_factors_loaded, 16)
            sp.dma_start(f1_sb[:, :, :], f1).then_inc(ffn_loaded, 16)
            sp.dma_start(conv_sb[:, :, :], conv).then_inc(ffn_loaded, 16)
            for i in range(BLOCKS):
                if i + 2 < BLOCKS:
                    sp.wait_ge(front_filled, i * USES + DC)
                    sp.dma_start((x_sb, rows)[i % 2][:, :, :], x_rows[:, (i + 2) * TILES:(i + 3) * TILES, :])\
                        .then_inc(x_loaded[i % 2], 16)
                for n in (DC + REP - 1, DC + REP):
                    sp.wait_ge(front_emptied[n % 2], i * (USES // 2) + emptied(n) + 1)
                sp.dma_start(q_dram[:, i * BB:(i + 1) * BB, :, :], q_stage[i % 2][:, :, :, :])\
                    .then_inc(q_stored[i % 2], 16)

            def load_near(i):
                for r in range(BT):
                    sp.dma_start(near[r * S:(r + 1) * S, :, 1:P + 1],
                                 x1_near[r, :, bass.ds(i * BB, BB), :]).then_inc(near_loaded, 16)

            def queries_and_keys(g):
                i, half = g // 2, g % 2
                if g >= 2:
                    sp.wait_ge(scores_ready, (i - 1) * PAIRS + (half + 1) * PAIRS // 2)
                sp.dma_start(q_t[:, half * HALF:(half + 1) * HALF, :, :],
                             q_dram[:, g * HALF:(g + 1) * HALF, :, :]).then_inc(q_loaded[half], 16)
                for k in range(G):
                    sp.dma_start(k_wide[k * HD:(k + 1) * HD, half, k, :, :],
                                 k_all[g * HD:(g + 1) * HD, k, :, :]).then_inc(k_loaded[half], 16)

            def store_x1(i, t):
                sp.wait_ge(front_emptied[t % 2], emptied(PROJECTED + i * TILES + t) + 1)
                sp.dma_start(x1_rows[:, i * TILES + t, :], rows[:, t, :]).then_inc(x1_stored[t], 16)

            sp.wait_ge(front_emptied[0], emptied(PROJECTED))
            sp.wait_ge(front_emptied[1], emptied(PROJECTED))
            sp.wait_ge(zeros_set, 2)
            for stored in q_stored:
                sp.wait_ge(stored, 16 * BLOCKS // 2)
            for g in range(2):
                queries_and_keys(g)
            sp.wait_ge(down_factors_cleared, 2)
            for dst, src in down_factor_loads:
                sp.dma_start(dst, src).then_inc(down_factors_loaded, 16)
            sp.dma_start(x_sb[:, :, :], x_rows[:, 0:TILES, :]).then_inc(x_reloaded, 16)
            for i in range(BLOCKS):
                if i + 1 < BLOCKS:
                    queries_and_keys(2 * i + 2)
                    store_x1(i, 0)
                    queries_and_keys(2 * i + 3)
                    sp.wait_ge(resid_ready, (i + 1) * TILES)
                    sp.dma_start(x_sb[:, :, :], x_rows[:, (i + 1) * TILES:(i + 2) * TILES, :])\
                        .then_inc(x_reloaded, 16)
                else:
                    for n in range(2):
                        sp.wait_ge(k_loaded[n], 16 * G * BLOCKS)
                    sp.wait_ge(v_spread, 4 * BT * BLOCKS)
                    for dst, src in f2_loads:
                        sp.dma_start(dst, src).then_inc(f2_loaded, 16)
                    for stored in x1_stored:
                        sp.wait_ge(stored, 16 * i)
                    store_x1(i, 0)
                    sp.wait_ge(scores_ready, BLOCKS * PAIRS)
                    load_near(0)
                for t in range(1, TILES):
                    store_x1(i, t)

            def load_rows(i):
                sp.dma_start(rows[:, :, :], x1_rows[:, bass.ds(i * TILES, TILES), :]).then_inc(x1_loaded, 16)

            def store_out(i):
                for t in range(TILES):
                    sp.wait_ge(out_ready, i * TILES + t + 1)
                    sp.dma_start(out_rows[:, bass.ds(i * TILES + t, 1), :],
                                 rows[:, t:t + 1, :]).then_inc(out_stored, 16)

            for stored in x1_stored:
                sp.wait_ge(stored, 16 * BLOCKS)
            load_rows(0)
            with sp.Fori(0, BLOCKS - 1) as i:
                sp.wait_ge(conv_filled, (i + 1) * BT)
                load_near(i + 1)
                store_out(i)
                sp.wait_ge(out_stored, (i + 1) * TILES * 16)
                load_rows(i + 1)
            store_out(BLOCKS - 1)
            sp.wait_ge(out_stored, 16 * TILES * BLOCKS)

        @block.gpsimd
        def _(pool):
            def stack(n, a, b, a_s, b_s, part):
                to, width = b_s.shape[1], a_s.shape[1]
                if n == 0:
                    return pool.tensor_copy(part[2 * S:3 * S, 0:width], a[2 * S:3 * S])
                if n == 1:
                    return pool.tensor_tensor(a_s[2 * S:3 * S], a[2 * S:3 * S],
                                              part[2 * S:3 * S, 0:width].bitcast(F32), ALU.subtract)
                if n == 2:
                    return pool.tensor_copy(part[S:2 * S, 0:to], b[S:2 * S, :])
                if n == 3:
                    return pool.tensor_tensor(b_s[S:2 * S, :], b[S:2 * S, :], part[S:2 * S, 0:to].bitcast(F32),
                                              ALU.subtract)
                if n == 4:
                    return pool.tensor_copy(a_s[0:2 * S], a[0:2 * S])
                if n == 5:
                    return pool.tensor_copy(b_s[0:S, :], b[0:S, :])
                return pool.tensor_copy(b_s[2 * S:3 * S, :], b[2 * S:3 * S, :])

            pool.memset(ones[:, :], 1.0).then_inc(ones_set, 1)
            pool.memset(mix[:, :, :, :], 0.0).then_inc(zeros_set, 1)
            pool.wait_ge(cond_loaded, 16 * len(cond_loads))
            pool.tensor_tensor(convb_terms[:, :, :], cond_sb[:, :].unsqueeze(2).to_broadcast([COND, B, S]),
                               convc_sb[:, :].unsqueeze(1).to_broadcast([COND, B, S]), ALU.mult)\
                .then_inc(terms_made, 1)
            pool.memset(k_wide[:, :, :, :, :], 0.0).then_inc(zeros_set, 1)
            pool.wait_ge(spread_pe, 9)
            pool.memset(a_up[:, :, :], 0.0).then_inc(up_factors_cleared, 1)
            pool.memset(b_up[:, :], 0.0).then_inc(up_factors_cleared, 1)
            pool.wait_ge(up_factors_loaded, 16 * len(up_factor_loads))
            for n in range(PARTS):
                if n:
                    pool.wait_ge(up_stacked, n)
                stack(n, a_up_rows, b_up, a_up_s_rows, b_up_s, up_part).then_inc(up_stacked, 1)
            pool.wait_ge(front_filled, PROJECTED)
            pool.memset(v_wide[:, :, :, :, :], 0.0).then_inc(v_cleared, 1)
            pool.wait_ge(front_emptied[0], emptied(PROJECTED))
            pool.wait_ge(front_emptied[1], emptied(PROJECTED))
            pool.memset(a_down[:, :], 0.0).then_inc(down_factors_cleared, 1)
            pool.memset(b_down[:, :], 0.0).then_inc(down_factors_cleared, 1)
            pool.wait_ge(spread_act, 9)

            def stack_down(s):
                if s == 0:
                    pool.wait_ge(down_factors_loaded, 16 * len(down_factor_loads))
                else:
                    pool.wait_ge(down_stacked, s)
                stack(s, a_down[:, :], b_down, a_down_s[:, :], b_down_s, down_part).then_inc(down_stacked, 1)

            def step(i, s, start, first):
                n = i * PAIRS + s
                if start:
                    pool.wait_ge(top_ready, n + 1)
                    pr = probs[:, s % PROBS].rearrange("p b g k -> p (b g) k")
                    pool.tensor_tensor(pr, pr, top[:, s % PROBS].unsqueeze(2).to_broadcast([P, 2 * G, S]),
                                       ALU.subtract).then_inc(shifted, 1)
                if (s >= 1 or not first) and s < PAIRS + 1:
                    pool.wait_ge(inv_ready, n)
                    pr = probs[:, (s - 1) % PROBS].rearrange("p b g k -> p (b g) k")
                    pool.tensor_tensor(pr, pr, inv[:, (s - 1) % PROBS].unsqueeze(2).to_broadcast([P, 2 * G, S]),
                                       ALU.mult).then_inc(probs_ready, 1)
                if start and s % 2:
                    t = s // 2
                    if t == 0:
                        pool.wait_ge(x_reloaded, (i + 1) * 16)
                    if not first:
                        pool.wait_ge(x1_stored[t], i * 16)
                    pool.tensor_tensor(rows[:, t, :].rearrange("p (r n) -> p r n", r=BT),
                                       x_sb[:, t, :].rearrange("p (n r) -> p r n", r=BT),
                                       bo_all[:, :].rearrange("p (r n) -> p r n", r=BT), ALU.add)\
                        .then_inc(resid_ready, 1)
                if first and s < PARTS:
                    pool.wait_ge(shifted, s + 1)
                    if s:
                        pool.wait_ge(probs_ready, s)
                    if start and s % 2:
                        pool.wait_ge(resid_ready, (s + 1) // 2)
                    stack_down(s)
                    pool.wait_ge(down_stacked, s + 1)
                if s == PAIRS:
                    pool.wait_ge(scores_ready, BLOCKS * PAIRS)
                    pool.memset(near[:, :, 0:1], 0.0).then_inc(near_zeroed, 1)
                    pool.memset(near[:, :, P + 1:P + 2], 0.0).then_inc(near_zeroed, 1)

            pipeline(pool, step)
            for h in range(HC):
                for n, (w, hi, lo) in enumerate(split_parts(h)):
                    pool.wait_ge(hi_split, 3 * h + n + 1)
                    pool.tensor_tensor(lo, w, hi.bitcast(F32), ALU.subtract).then_inc(lo_split, 1)

        @block.scalar
        def _(act):
            act.dma_start(x_sb[:, :, :], x_rows[:, 0:TILES, :]).then_inc(x_loaded[0], 16)
            act.dma_start(rows[:, :, :], x_rows[:, TILES:2 * TILES, :]).then_inc(x_loaded[1], 16)
            for dst, src in attn_loads:
                act.dma_start(dst, src).then_inc(attn_loaded, 16)
            act.wait_ge(cond_loaded, 16 * len(cond_loads))
            act.wait_ge(cond_pe, 1)
            act.activation(hid0[:, :], ps[0][:, 0:B], ACT.Gelu, bias=b0_sb[:, 0:1]).then_inc(cond_act, 1)
            act.wait_ge(cond_pe, 2)
            act.activation(hid1[:, :], ps[1][:, 0:B], ACT.Gelu, bias=b1_sb[:, 0:1]).then_inc(cond_act, 1)
            act.wait_ge(cond_dve, 1)
            act.activation(att[:, :], ps[2][0:B, 0:K], ACT.Exp, bias=neg_top[:, 0:1],
                           accum_out=att_sum[:, 0:1]).then_inc(cond_act, 1)
            for n in range(9):
                act.wait_ge(spread_pe, n + 1)
                dst = (mixb_all[:, n * 512:(n + 1) * 512] if n < 4 else
                       convb_all[:, (n - 4) * 512:(n - 3) * 512] if n < 8 else bo_all[:, :])
                act.copy(dst, ps[4 + n % 2][:, :]).then_inc(spread_act, 1)
            with act.Fori(0, BLOCKS // 2) as i:
                for half in range(2):
                    use = (2 * i + half) * USES
                    n = DC
                    act.wait_ge(front_filled, use + n + 1)
                    act.copy(k_all[:, :, bass.ds((2 * i + half) * 2, 2), :].rearrange("p g c s -> p c g s"),
                             front[n % 2][:, :].rearrange("p (c g s) -> p c g s", c=2, s=S))\
                        .then_inc(front_emptied[n % 2], 1)
                    for j in range(REP):
                        n = DC + 1 + j
                        act.wait_ge(front_filled, use + n + 1)
                        act.copy(q_stage[half][:, :, j, :],
                                 front[n % 2][:, :].rearrange("p (b s) -> p b s", s=S))\
                            .then_inc(front_emptied[n % 2], 1)
                    n = DC + 1 + REP
                    act.wait_ge(front_filled, use + n + 1)
                    act.copy(v_all[:, bass.ds((2 * i + half) * TILES, TILES), :],
                             front[n % 2][:, :].rearrange("p (t c) -> p t c", t=TILES))\
                        .then_inc(front_emptied[n % 2], 1)
                for stored in q_stored:
                    act.wait_ge(stored, 16 * (i + 1))

            def step(i, s, start, first):
                n = i * PAIRS + s
                if (s >= TURN or not first) and s - TURN < PAIRS:
                    act.wait_ge(turned, n - TURN + 1)
                    act.copy(probs_t[:, (s - TURN) % 2], turn_bank[(s - TURN) % 2][:, :]
                             .rearrange("p (c q) -> p c q", q=P)).then_inc(turned_copied, 1)
                if (s >= CONTEXT or not first) and s - CONTEXT < PAIRS:
                    q = (s - CONTEXT) % PAIRS
                    act.wait_ge(ctx_filled, n - CONTEXT + 1)
                    act.copy(ctx_t[:, :, q * 2 * S:(q + 1) * 2 * S].rearrange("p j (b s) -> p b j s", s=S),
                             ctx_bank[q % 2][:, 0:2 * P].rearrange("p (b j s) -> p b j s", b=2, j=REP))\
                        .then_inc(ctx_copied, 1)
                if start:
                    act.wait_ge(shifted, n + 1)
                    act.activation(probs[:, s % PROBS], probs[:, s % PROBS], ACT.Exp, scale=SCALE)\
                        .then_inc(exp_ready, 1)

            pipeline(act, step)

            def split(h):
                for n, (w, hi, lo) in enumerate(split_parts(h)):
                    if n == 2:
                        act.wait_ge(down_folded, h + 1)
                    act.copy(hi, w).then_inc(hi_split, 1)

            def round_conv(i):
                for n, q in enumerate(conv_order):
                    act.wait_ge(c_ready, i * BT + n + 1)
                    act.copy(c_hi[:, :, q * P:(q + 1) * P].rearrange("p s (b o) -> p b s o", o=S),
                             c_raw[n % 2][:, :, :, :]).then_inc(c_hi_ready, 1)

            def block_of_rows(i, first, more):
                for h, w in enumerate(HW):
                    act.wait_ge(up1_filled, i * HC + h + 1)
                    if h >= 2 or not first:
                        act.wait_ge(gate_lo_ready, i * HC + max(h - 1, 0))
                    act.activation(gate[0:w, h % 2, :], up_bank[2 * (h % 2)][0:w, :], ACT.Silu)\
                        .then_inc(silu_ready, 1)
                    act.wait_ge(gate_ready, i * HC + h + 1)
                    act.copy(gate_hi[0:w, h % 2, :], gate[0:w, h % 2, :]).then_inc(gate_hi_ready, 1)
                    if first and h + 2 < HC:
                        split(h + 2)
                if more:
                    round_conv(i + 1)

            act.wait_ge(up_folded, FOLDS)
            act.wait_ge(scores_ready, BLOCKS * PAIRS)
            act.wait_ge(front_filled, PROJECTED + BLOCKS * TILES)
            round_conv(0)
            for h in range(2):
                split(h)
            blocks(act, block_of_rows)

        @block.vector
        def _(dve):
            dve.wait_ge(cond_pe, 3)
            dve.tensor_reduce(neg_top[:, :], ps[2][0:B, 0:K], AX_X, ALU.max, negate=True).then_inc(cond_dve, 1)
            dve.wait_ge(cond_act, 3)
            dve.reciprocal(att_inv[:, :], att_sum[:, :]).then_inc(cond_dve, 1)
            dve.wait_ge(cond_dve, 2)
            dve.tensor_scalar(att[:, :], att[:, :], att_inv[:, 0:1], None, ALU.mult).then_inc(cond_dve, 1)
            dve.wait_ge(cond_pe, 4)
            dve.tensor_copy(att_t[:, :], ps[3][0:K, 0:B]).then_inc(cond_dve, 1)
            dve.tensor_copy(convb_row[:, :, :], convb_sb[:, :].unsqueeze(1).to_broadcast([1, BB, S]))\
                .then_inc(terms_made, 1)
            dve.wait_ge(cond_dve, 4)
            dve.tensor_tensor(mixb_terms[:, :, :], att_t[:, :].unsqueeze(2).to_broadcast([K, B, S]),
                              mixb_sb[:, :].unsqueeze(1).to_broadcast([K, B, S]), ALU.mult)\
                .then_inc(terms_made, 1)
            dve.wait_ge(zeros_set, 1)
            for n in range(4):
                dve.wait_ge(cond_pe, 5 + n)
                made = ps[n][:, :].rearrange("p (o t c) -> p t o c", o=8, c=BT)
                for c in range(BT):
                    copy = dve.tensor_copy(mix[c * S:(c + 1) * S, :, c, n * 8:(n + 1) * 8],
                                           made[c * S:(c + 1) * S, :, :, c])
                copy.then_inc(front_emptied[n] if n < 2 else mix_made, 1)
            dve.wait_ge(spread_act, 9)
            with dve.Fori(0, BLOCKS // 2) as i:
                for half in range(2):
                    for c in range(DC):
                        dve.wait_ge(front_filled, (2 * i + half) * USES + c + 1)
                        dve.tensor_tensor(y_t[half][:, c, :], front[c % 2][:, :],
                                          mixb_all[:, bass.ds((2 * i + half) * BLOCK, BLOCK)], ALU.add)\
                            .then_inc(front_emptied[c % 2], 1)
                for n, (f, c, _) in enumerate(2 * up_folds):
                    dst = f[:, c, bass.ds((2 * i + n // len(up_folds)) * FOLD_N, FOLD_N)]
                    dve.wait_ge(up_fold_filled, i * (FOLDS // 2) + n + 1)
                    dve.scalar_tensor_tensor(out=dst, in0=fold_bank[n % 4][:, 0:FOLD_N], scalar=LORA_SCALE,
                                             in1=dst, op0=ALU.mult, op1=ALU.add).then_inc(up_folded, 1)
            dve.wait_ge(attn_loaded, 16 * len(attn_loads))
            dve.wait_ge(front_emptied[1], emptied(PROJECTED))
            dve.wait_ge(v_cleared, 1)

            def spread_values(i, half):
                vg = v_all[:, :, :].rearrange("p (c h) (g d) -> p c h g d", h=2, d=HD)
                vw = v_wide[:, half * HALF:(half + 1) * HALF, :, :, :].rearrange("p c h (z g) d -> p c h z g d", z=2)
                for g in range(BT):
                    for h in range(2):
                        dve.tensor_copy(vw[g * S:(g + 1) * S, :, h, h, g, :],
                                        vg[g * S:(g + 1) * S, :, h, bass.ds(2 * i + half, 1), :]
                                        .rearrange("p c g d -> p c (g d)")).then_inc(v_spread, 1)

            def step(i, s, start, first):
                n = i * PAIRS + s
                if start:
                    pr = probs[:, s % PROBS].rearrange("p b g k -> p (b g) k")
                    dve.wait_ge(scores_ready, n + 1)
                    if s >= PROBS or not first:
                        dve.wait_ge(turned, n - PROBS + 1)
                    dve.tensor_tensor(pr, score_bank[s % 2][:, :].rearrange("p (c k) -> p c k", k=S),
                                      causal_sb[:, :].unsqueeze(1).to_broadcast([P, 2 * G, S]), ALU.add)\
                        .then_inc(masked, 1)
                    dve.wait_ge(masked, n + 1)
                    dve.tensor_reduce(top[:, s % PROBS, :], pr, AX_X, ALU.max).then_inc(top_ready, 1)
                if (s >= 1 or not first) and s < PAIRS + 1:
                    q = (s - 1) % PROBS
                    dve.wait_ge(exp_ready, n)
                    dve.tensor_reduce(total[:, q, :], probs[:, q].rearrange("p b g k -> p (b g) k"),
                                      AX_X, ALU.add).then_inc(sum_ready, 1)
                    dve.wait_ge(sum_ready, n)
                    dve.reciprocal(inv[:, q, :], total[:, q, :]).then_inc(inv_ready, 1)
                if start and s == 0:
                    if not first:
                        dve.wait_ge(ctx_filled, i * PAIRS - PAIRS // 2)
                    spread_values(i, 0)
                if start and s == CONTEXT:
                    if not first:
                        dve.wait_ge(ctx_filled, i * PAIRS)
                    spread_values(i, 1)
                if s % 2 == 0 and (s >= OUT or not first):
                    t = (s - OUT) // 2 % TILES
                    tile = i * TILES + (s - OUT) // 2
                    dve.wait_ge(front_filled, PROJECTED + tile + 1)
                    dve.wait_ge(resid_ready, tile + 1)
                    dve.tensor_tensor(rows[:, t, :], front[t % 2][:, :], rows[:, t, :], ALU.add)\
                        .then_inc(front_emptied[t % 2], 1)

            pipeline(dve, step)

            def fold_down(h):
                dst = f2_sb[0:HW[h], h, :]
                dve.wait_ge(down_fold_filled, h + 1)
                dve.scalar_tensor_tensor(out=dst, in0=fold_bank[h % 4][0:HW[h], :], scalar=LORA_SCALE,
                                         in1=dst, op0=ALU.mult, op1=ALU.add).then_inc(down_folded, 1)

            def conv_lo(i, n):
                q = conv_order[n]
                dve.wait_ge(c_hi_ready, i * BT + n + 1)
                dve.tensor_tensor(c_lo[:, :, q * P:(q + 1) * P].rearrange("p s (b o) -> p b s o", o=S),
                                  c_raw[n % 2][:, :, :, :],
                                  c_hi[:, :, q * P:(q + 1) * P].rearrange("p s (b o) -> p b s o", o=S).bitcast(F32),
                                  ALU.subtract).then_inc(c_lo_ready, 1)

            def copy_conv(i, first=False):
                for n, q in enumerate(conv_order):
                    dve.wait_ge(conv_filled, i * BT + n + 1)
                    if n >= 2:
                        dve.wait_ge(c_lo_ready, i * BT + n - 1)
                    cb = convb_all[:, bass.ds(i * BLOCK + q * P, P)].rearrange("p (b o) -> p b o", o=S)
                    dve.tensor_tensor(c_raw[n % 2][:, :, :, :],
                                      up_bank[q][:, :].rearrange("p (b s o) -> p b s o", s=DC, o=S),
                                      cb.unsqueeze(2).to_broadcast([P, BT, DC, S]), ALU.add)\
                        .then_inc(c_ready, 1)
                    if n:
                        conv_lo(i, n - 1)
                    if first:
                        for h in range(3 * n, min(3 * n + 3, HC)):
                            fold_down(h)
                conv_lo(i, BT - 1)

            def block_of_rows(i, first, more):
                for h, w in enumerate(HW):
                    dve.wait_ge(up3_filled, i * HC + h + 1)
                    dve.wait_ge(silu_ready, i * HC + h + 1)
                    dve.tensor_tensor(gate[0:w, h % 2, :], up_bank[2 * (h % 2) + 1][0:w, :], gate[0:w, h % 2, :],
                                      ALU.mult).then_inc(gate_ready, 1)
                    dve.wait_ge(gate_hi_ready, i * HC + h + 1)
                    dve.tensor_tensor(gate_lo[0:w, h % 2, :], gate[0:w, h % 2, :],
                                      gate_hi[0:w, h % 2, :].bitcast(F32), ALU.subtract).then_inc(gate_lo_ready, 1)
                if more:
                    copy_conv(i + 1)
                dve.wait_ge(x1_loaded, 16 * (i + 1))
                for t in range(TILES):
                    dve.wait_ge(down_filled, i * TILES + t + 1)
                    dve.tensor_tensor(rows[:, t, :], down_bank[t][:, :], rows[:, t, :], ALU.add)\
                        .then_inc(out_ready, 1)

            dve.wait_ge(ctx_filled, BLOCKS * PAIRS)
            dve.wait_ge(front_filled, PROJECTED + BLOCKS * TILES)
            copy_conv(0, first=True)
            blocks(dve, block_of_rows)

        @block.tensor
        def _(pe):
            pe.wait_ge(cond_loaded, 16 * len(cond_loads))
            pe.matmul(ps[0][:, 0:B], w0_sb[:, :], cond_sb[:, :], start=True, stop=True).then_inc(cond_pe, 1)
            pe.wait_ge(cond_act, 1)
            pe.matmul(ps[1][:, 0:B], w1_sb[:, :], hid0[:, :], start=True, stop=True).then_inc(cond_pe, 1)
            pe.wait_ge(ones_set, 1)
            pe.wait_ge(cond_act, 2)
            pe.matmul(ps[2][0:B, 0:K], hid1[:, :], w2_sb[:, :], start=True, stop=False)
            pe.matmul(ps[2][0:B, 0:K], ones[0:1, 0:B], b2_sb[:, :], start=False, stop=True).then_inc(cond_pe, 1)
            pe.wait_ge(cond_dve, 3)
            pe.transpose(ps[3][0:K, 0:B], att[:, :], ident_sb[0:B, 0:B]).then_inc(cond_pe, 1)
            pe.wait_ge(cond_dve, 4)
            for o in range(S):
                mm = pe.matmul(ps[o // 8][:, (o % 8) * B:(o % 8 + 1) * B],
                               mixw_sb[:, o, :, :].rearrange("k c i -> k (c i)"), att_t[:, :],
                               start=True, stop=True)
                if o % 8 == 7:
                    mm.then_inc(cond_pe, 1)
            pe.wait_ge(terms_made, 3)
            for n in range(9):
                if n >= 2:
                    pe.wait_ge(spread_act, n - 1)
                bank = ps[4 + n % 2][:, :]
                if n < 4:
                    rhs = mixb_terms[:, n * BB:(n + 1) * BB, :].rearrange("k b o -> k (b o)")
                    pe.matmul(bank, ones[0:K, :], rhs, start=True, stop=True).then_inc(spread_pe, 1)
                elif n < 8:
                    rhs = convb_terms[:, (n - 4) * BB:(n - 3) * BB, :].rearrange("k b o -> k (b o)")
                    pe.matmul(bank, ones[:, :], rhs, start=True, stop=False)
                    pe.matmul(bank, ones[0:1, :], convb_row[:, :, :].rearrange("k b o -> k (b o)"),
                              start=False, stop=True).then_inc(spread_pe, 1)
                else:
                    pe.matmul(bank, ones[0:1, :], bo_sb[:, :], start=True, stop=True).then_inc(spread_pe, 1)
            pe.wait_ge(front_emptied[0], emptied(0))
            pe.wait_ge(front_emptied[1], emptied(1))
            pe.wait_ge(mix_made, 2)
            pe.wait_ge(attn_loaded, 16 * len(attn_loads))
            pe.wait_ge(spread_act, 9)

            def fold_up(i, m):
                if m == 0:
                    pe.wait_ge(up_stacked, PARTS)
                    pe.wait_ge(ffn_loaded, 16 * 3)
                if m >= 4:
                    pe.wait_ge(up_folded, i * (FOLDS // 2) + m - 3)
                _, c, factor = up_folds[m % len(up_folds)]
                pe.matmul(fold_bank[m % 4][:, 0:FOLD_N], a_up_s[:, factor, c * P:(c + 1) * P],
                          b_up_s[:, bass.ds((2 * i + m // len(up_folds)) * FOLD_N, FOLD_N)],
                          start=True, stop=True).then_inc(up_fold_filled, 1)

            with pe.Fori(0, BLOCKS // 2) as i:
                for half, buf in enumerate((x_sb, rows)):
                    blk = 2 * i + half

                    def bank_free(n):
                        pe.wait_ge(front_emptied[n % 2], blk * (USES // 2) + emptied(n))

                    pe.wait_ge(x_loaded[half], 16 * (i + 1))
                    for c in range(DC):
                        bank_free(c)
                        for t in range(TILES):
                            mm = pe.matmul(front[c % 2][:, t * P:(t + 1) * P], buf[:, t, c * P:(c + 1) * P],
                                           mix[:, bass.ds(blk * TILES + t, 1), :, :]
                                           .rearrange("p t c o -> p (t c o)"), start=True, stop=True)
                        mm.then_inc(front_filled, 1)
                    bank_free(DC + 1)
                    for n in range(DC, DC + 1 + REP):
                        bank_free(n)
                        for c in range(DC):
                            w = wk_sb[:, c, :] if n == DC else wq_sb[:, c, n - DC - 1, :]
                            mm = pe.matmul(front[n % 2][:, :], w, y_t[half][:, c, :],
                                           start=(c == 0), stop=(c == DC - 1))
                        mm.then_inc(front_filled, 1)
                        if half == 1 and n > DC:
                            for m in range((n - DC - 1) * TILES, (n - DC) * TILES):
                                fold_up(i, m)
                    n = DC + 1 + REP
                    bank_free(n)
                    for t in range(TILES):
                        for c in range(DC):
                            mm = pe.matmul(front[n % 2][:, t * P:(t + 1) * P], y_t[half][:, c, t * P:(t + 1) * P],
                                           wv_sb[:, c, :], start=(c == 0), stop=(c == DC - 1))
                    mm.then_inc(front_filled, 1)
                pe.wait_ge(up_folded, (i + 1) * (FOLDS // 2))

            def step(i, s, start, first):
                n = i * PAIRS + s
                if start:
                    if s % (PAIRS // 2) == 0:
                        half = s // (PAIRS // 2)
                        pe.wait_ge(q_loaded[half], (i + 1) * 16)
                        pe.wait_ge(k_loaded[half], (i + 1) * G * 16)
                    if s >= 2 or not first:
                        pe.wait_ge(masked, n - 1)
                    for b in range(2):
                        c = 2 * s + b
                        mm = pe.matmul(score_bank[s % 2][:, b * G * S:(b + 1) * G * S],
                                       q_t[:, c, :, :].rearrange("p j s -> p (j s)"),
                                       k_wide[:, c // HALF, :, c % HALF, :], start=True, stop=True)
                    mm.then_inc(scores_ready, 1)
                if (s >= TURN or not first) and s - TURN < PAIRS:
                    q = s - TURN
                    pe.wait_ge(probs_ready, n - TURN + 1)
                    if q >= 2 or not first:
                        pe.wait_ge(turned_copied, n - TURN - 1)
                    for b in range(2):
                        for h in range(2):
                            mm = pe.transpose(turn_bank[q % 2][:, (2 * b + h) * P:(2 * b + h + 1) * P],
                                              probs[:, q % PROBS, b, 4 * h:4 * h + 4, :].rearrange("p g k -> p (g k)"),
                                              ident_sb[:, :])
                    mm.then_inc(turned, 1)
                if (s >= CONTEXT or not first) and s - CONTEXT < PAIRS:
                    q = (s - CONTEXT) % PAIRS
                    if q % (PAIRS // 2) == 0:
                        half = (s - CONTEXT) // (PAIRS // 2)
                        pe.wait_ge(v_spread, (2 * i + half + 1) * 2 * BT)
                    pe.wait_ge(turned_copied, n - CONTEXT + 1)
                    if s - CONTEXT >= 2 or not first:
                        pe.wait_ge(ctx_copied, n - CONTEXT - 1)
                    for b in range(2):
                        for h in range(2):
                            mm = pe.matmul(ctx_bank[q % 2][:, b * P:(b + 1) * P],
                                           v_wide[:, 2 * q + b, h].rearrange("p g d -> p (g d)"),
                                           probs_t[:, q % 2, 2 * b + h, :], start=(h == 0), stop=(h == 1))
                    mm.then_inc(ctx_filled, 1)
                if s % 2 == 0 and (s >= OUT or not first):
                    t = (s - OUT) // 2 % TILES
                    tile = i * TILES + (s - OUT) // 2
                    pe.wait_ge(ctx_copied, n - OUT + 2)
                    pe.wait_ge(front_emptied[t % 2], emptied(PROJECTED) + i * (TILES // 2) + (s - OUT) // 2 // 2)
                    for j in range(REP):
                        mm = pe.matmul(front[t % 2][:, :], ctx_t[:, j, t * P:(t + 1) * P], wo_sb[:, j, :],
                                       start=(j == 0), stop=(j == REP - 1))
                    mm.then_inc(front_filled, 1)

            pipeline(pe, step)

            def convolve(i, first=False):
                pe.wait_ge(near_loaded, 16 * BT * (i + 1))
                for n, q in enumerate(conv_order):
                    if not first:
                        pe.wait_ge(gate_ready, i * HC - (1 if q >= 2 else 0))
                    elif q < 2:
                        pe.wait_ge(front_emptied[q], emptied(PROJECTED + BLOCKS * TILES))
                    for b in range(BT):
                        for m in range(NEAR):
                            mm = pe.matmul(up_bank[q][:, b * P:(b + 1) * P], near[:, q * BT + b, m:m + P],
                                           conv_sb[:, m, :], start=(m == 0), stop=(m == NEAR - 1))
                    mm.then_inc(conv_filled, 1)
                    if first:
                        for h in range(3 * n, min(3 * n + 3, HC)):
                            fold_down(h)

            def fold_down(h):
                if h >= 4:
                    pe.wait_ge(down_folded, h - 3)
                pe.matmul(fold_bank[h % 4][0:HW[h], :], a_down_s[:, h * P:h * P + HW[h]], b_down_s[:, :],
                          start=True, stop=True).then_inc(down_fold_filled, 1)

            def up(i, h, first):
                w, cols = HW[h], slice(h * P, h * P + HW[h])
                if first:
                    pe.wait_ge(lo_split, 3 * h + 2)
                if h >= 2:
                    pe.wait_ge(gate_ready, i * HC + h - 1)
                for parts, bank, filled in (
                        (((f1_hi[:, :, cols], c_hi), (f1_hi[:, :, cols], c_lo), (f1_lo[:, :, cols], c_hi)),
                         up_bank[2 * (h % 2)], up1_filled),
                        (((f3_hi[:, h, :, 0:w], c_hi), (f3_hi[:, h, :, 0:w], c_lo), (f3_lo[:, :, cols], c_hi)),
                         up_bank[2 * (h % 2) + 1], up3_filled)):
                    for n, (f, c_part) in enumerate(parts):
                        for c in range(DC):
                            mm = pe.matmul(bank[0:w, :], f[:, c, :], c_part[:, c, :],
                                           start=(n == 0 and c == 0), stop=(n == 2 and c == DC - 1))
                    mm.then_inc(filled, 1)

            def down(i, h, first):
                w = HW[h]
                if first:
                    pe.wait_ge(lo_split, 3 * h + 3)
                pe.wait_ge(gate_lo_ready, i * HC + h + 1)
                if h == 0 and not first:
                    pe.wait_ge(out_ready, i * TILES)
                for t in range(TILES):
                    for n, (g, f) in enumerate(((gate_hi, f2_hi(h)), (gate_hi, f2_lo[0:w, h, :]),
                                                (gate_lo, f2_hi(h)))):
                        mm = pe.matmul(down_bank[t][:, :], g[0:w, h % 2, t * P:(t + 1) * P], f,
                                       start=(h == 0 and n == 0), stop=(h == HC - 1 and n == 2))
                    if h == HC - 1:
                        mm.then_inc(down_filled, 1)

            def block_of_rows(i, first, more):
                pe.wait_ge(c_lo_ready, BT * (i + 1))
                up(i, 0, first)
                for h in range(1, HC - 1):
                    up(i, h, first)
                    down(i, h - 1, first)
                up(i, HC - 1, first)
                if more:
                    convolve(i + 1)
                down(i, HC - 2, first)
                down(i, HC - 1, first)

            pe.wait_ge(near_zeroed, 2)
            pe.wait_ge(down_stacked, PARTS)
            pe.wait_ge(f2_loaded, 16 * len(f2_loads))
            pe.wait_ge(ctx_copied, BLOCKS * PAIRS)
            convolve(0, first=True)
            pe.wait_ge(down_folded, HC)
            blocks(pe, block_of_rows)


def layouts(a):
    perm = lambda w: w.reshape(*w.shape[:-1], P, BT).swapaxes(-1, -2).reshape(w.shape)
    wkv = a["L0_attn_Wkv"].reshape(DC, P, G, 2, HD)
    conv = np.zeros((BT, S, NEAR, BT, S), a["L0_cond2_weight"].dtype)
    for m in range(NEAR):
        for r in range(BT):
            for s in range(BT):
                tap = BT * (m - 1) + r - s + TAPS // 2
                if 0 <= tap < TAPS:
                    for co in range(S):
                        first = co // CG * CG
                        conv[r, first:first + CG, m, s, co] = a["L0_cond2_weight"][co, :, tap]
    t = lambda w: w.swapaxes(-1, -2)
    return {
        "x": a["x"].reshape(N, D), "cond_t": t(a["cond_128"]),
        "w0": a["L0_cond_W0"], "b0": a["L0_cond_b0"].reshape(COND, 1),
        "w1": a["L0_cond_W1"], "b1": a["L0_cond_b1"].reshape(COND, 1),
        "w2": a["L0_cond_W2"], "b2": a["L0_cond_b2"].reshape(1, K),
        "mix_w": a["L0_cond_weight"].reshape(K, S, S), "mix_b": a["L0_cond_bias_k"],
        "wq": a["L0_attn_Wq"].reshape(DC, P, G, REP, HD).transpose(1, 0, 3, 2, 4).reshape(P, DC, REP, GD),
        "wk": wkv[:, :, :, 0].transpose(1, 0, 2, 3).reshape(P, DC, GD),
        "wv": wkv[:, :, :, 1].transpose(1, 0, 2, 3).reshape(P, DC, GD),
        "wo": perm(a["L0_attn_Wo"].reshape(G, REP, HD, D).transpose(0, 2, 1, 3)).reshape(GD, REP, D),
        "bo": perm(a["L0_attn_bo"].reshape(1, D)),
        "conv": conv.reshape(P, NEAR, P), "conv_cond": t(a["L0_cond2_c_weight"]),
        "conv_bias": a["fside_S_0"].reshape(1, S),
        "f1": a["L0_ffn_w1"].reshape(HID, P, BT).transpose(1, 2, 0),
        "f3": a["L0_ffn_w3"].reshape(HID, P, BT).transpose(1, 2, 0),
        "f2": perm(t(a["L0_ffn_w2"])),
        "a1": perm(a["L0_ffn_lora_A1"]), "a3": perm(a["L0_ffn_lora_A3"]), "a2": a["L0_ffn_lora_A2"],
        "lb1": t(a["L0_ffn_lora_B1"]), "lb3": t(a["L0_ffn_lora_B3"]), "lb2": perm(t(a["L0_ffn_lora_B2"])),
        "ident": np.eye(P, dtype=np.float32),
        "causal": np.where(np.arange(S)[None, :] > np.arange(P)[:, None] % S, -1e30, 0.0).astype(np.float32),
    }


def kernel(**inputs):
    import concourse.bacc as bacc
    from concourse.bass_utils import run_bass_kernel_spmd

    nc = bacc.Bacc("TRN2", target_bir_lowering=False, num_devices=1)
    arrays = {f"in_{k}": np.ascontiguousarray(v) for k, v in
              layouts({k: np.asarray(v) for k, v in inputs.items()}).items()}
    args = {k[3:]: nc.dram_tensor(k, v.shape, mybir.dt.from_np(v.dtype), kind="ExternalInput").ap()
            for k, v in arrays.items()}
    out = nc.dram_tensor("out", (N, D), F32, kind="ExternalOutput").ap()
    adaln_attention_ffn(nc, out=out, **args)
    r = run_bass_kernel_spmd(nc, [arrays], core_ids=[0])
    got = r.results[0]["out"]
    return got.reshape(B, S, BT, P).swapaxes(2, 3).reshape(B, S, D)
```

```python
from contextlib import ExitStack

import numpy as np

import concourse.bass as bass
from concourse import mybir

F32 = mybir.dt.float32
F32R = mybir.dt.float32r
ALU = mybir.AluOpType
ACT = mybir.ActivationFunctionType
AX_X = mybir.AxisListType.X

P = 128
B, S, D = 64, 32, 512
N = B * S
COND = 128
K = 8
G, REP, HD = 8, 4, 16
GD = G * HD
TAPS, CG = 9, 8
HID, R = 1376, 16
LORA_SCALE = 2.0
BLOCK = 512
BLOCKS = N // BLOCK
TILES = BLOCK // P
BB = BLOCK // S
BT = P // S
PAIRS = BB // 2
DC = D // P
HC = -(-HID // P)
HW = [min(P, HID - h * P) for h in range(HC)]
NEAR = 3
SCALE = HD ** -0.5
FOLD_N = HID // BLOCKS
STACK = 3 * S
QG = B // G
HALF = BB // 2
USES = DC + 1 + REP + 1
PROJECTED = USES * BLOCKS
PARAMS = {"cond_t": B, "w0": COND, "b0": 1, "w1": COND, "b1": 1, "w2": K, "b2": K, "conv_cond": S,
          "conv_bias": S, "mix_w": S * S, "mix_b": S}
PROBS = 4
TURN = 3
CONTEXT = TURN + 1
OUT = CONTEXT + 2
FOLDS = 2 * DC * BLOCKS
F2_HEAD = 8


def adaln_attention_ffn(nc, x, params, wq, wk, wv, wo, bo, conv, f1, f3, f2, up_factors, down_factors,
                        ident, causal, out):
    with ExitStack() as ctx:
        def sb(name, shape, stage=ctx, dtype=F32):
            return stage.enter_context(nc.sbuf_tensor(name, shape, dtype))

        def sem(name):
            return ctx.enter_context(nc.semaphore(name))

        ident_sb = sb("ident_sb", [P, P])
        causal_sb = sb("causal_sb", [P, S])
        ones = sb("ones", [1, B])
        conv_sb = sb("conv_sb", [P, NEAR, P])
        neg_top = sb("neg_top", [B, 1])
        att = sb("att", [B, K])
        att_sum = sb("att_sum", [B, 1])
        att_inv = sb("att_inv", [B, 1])
        convb_sb = sb("convb_sb", [B, S])
        mixb_sb = sb("mixb_sb", [B, S])
        convb_all = sb("convb_all", [P, N])
        bo_all = sb("bo_all", [P, D])

        ps = [ctx.enter_context(nc.psum_tensor(f"ps{n}", [P, 512], F32)) for n in range(8)]

        cond_loaded = sem("cond_loaded")
        ident_loaded = sem("ident_loaded")
        mix_loaded = sem("mix_loaded")
        attn_loaded = sem("attn_loaded")
        ffn_loaded = sem("ffn_loaded")
        f2_loaded = sem("f2_loaded")
        x_loaded = [sem("x_loaded"), sem("x_loaded_in_rows")]
        ones_set = sem("ones_set")
        warmed = sem("warmed")
        zeros_set = sem("zeros_set")
        cond_pe = sem("cond_pe")
        cond_act = sem("cond_act")
        cond_dve = sem("cond_dve")
        mix_made = sem("mix_made")
        shifts_pe = sem("shifts_pe")
        wkq_hi_split = sem("wkq_hi_split")
        wkq_lo_split = sem("wkq_lo_split")
        y_hi_ready = sem("y_hi_ready")
        y_lo_ready = sem("y_lo_ready")
        wo_loaded = sem("wo_loaded")
        wo_hi_split = sem("wo_hi_split")
        wo_lo_split = sem("wo_lo_split")
        ctx_lo_ready = sem("ctx_lo_ready")
        shifts_act = sem("shifts_act")
        conv_shift_stored = sem("conv_shift_stored")
        mix_shift_stored = sem("mix_shift_stored")
        conv_shift_spread = sem("conv_shift_spread")
        mix_shift_spread = [sem("first_mix_shift_spread"), sem("mix_shift_spread")]
        bo_spread = sem("bo_spread")
        causal_loaded = sem("causal_loaded")
        front_filled = sem("front_filled")
        front_emptied = [sem("front0_emptied"), sem("front1_emptied")]
        v_cleared = sem("v_cleared")
        q_stored = [sem(f"q_block{n}_stored") for n in range(2)]
        up_factors_loaded = sem("up_factors_loaded")
        up_stacked = sem("up_stacked")
        up_lo_stacked = sem("up_lo_stacked")
        down_factors_loaded = sem("down_factors_loaded")
        down_stacked = sem("down_stacked")
        down_lo_stacked = sem("down_lo_stacked")
        up_folded = sem("up_folded")
        hi_split = sem("hi_split")
        lo_split = sem("lo_split")
        c_ready = sem("c_ready")
        c_hi_ready = sem("c_hi_ready")
        c_lo_ready = sem("c_lo_ready")
        gate_hi_ready = sem("gate_hi_ready")
        gate_lo_ready = sem("gate_lo_ready")
        q_loaded = [sem(f"q_half{n}_loaded") for n in range(2)]
        k_loaded = [sem(f"k_half{n}_loaded") for n in range(2)]
        v_spread = sem("v_spread")
        scores_ready = sem("scores_ready")
        masked = sem("masked")
        top_ready = sem("top_ready")
        shifted = sem("shifted")
        exp_ready = sem("exp_ready")
        sum_ready = sem("sum_ready")
        inv_ready = sem("inv_ready")
        probs_ready = sem("probs_ready")
        turned = sem("turned")
        turned_copied = sem("turned_copied")
        ctx_filled = sem("ctx_filled")
        ctx_copied = sem("ctx_copied")
        x_reloaded = sem("x_reloaded")
        resid_ready = sem("resid_ready")
        x1_stored = [sem(f"x1_tile{t}_stored") for t in range(TILES)]
        up_fold_filled = sem("up_fold_filled")
        down_fold_filled = sem("down_fold_filled")
        down_folded = sem("down_folded")
        near_zeroed = sem("near_zeroed")
        near_loaded = sem("near_loaded")
        x1_loaded = sem("x1_loaded")
        conv_filled = sem("conv_filled")
        up1_filled = sem("up1_filled")
        up3_filled = sem("up3_filled")
        silu_ready = sem("silu_ready")
        gate_ready = sem("gate_ready")
        down_filled = sem("down_filled")
        out_ready = sem("out_ready")
        out_stored = sem("out_stored")

        x1_dram = nc.dram_tensor("x1_dram", [N, D], F32).ap()
        shifts_dram = nc.dram_tensor("shifts_dram", [2, B, S], F32).ap()
        q_dram = nc.dram_tensor("q_dram", [GD, B, REP, S], F32).ap()

        rows = sb("rows", [P, TILES, D])
        top = sb("top", [P, PROBS, 2 * G])
        total = sb("total", [P, PROBS, 2 * G])
        inv = sb("inv", [P, PROBS, 2 * G])
        with ExitStack() as room:
            wk_sb = sb("wk_sb", [P, DC, GD], room)
            wv_sb = sb("wv_sb", [P, DC, GD], room)
            mix = sb("mix", [P, N // P, BT, S], room)
            mixb_all = sb("mixb_all", [P, N], room)
        with ExitStack() as room:
            wk_lo = sb("wk_lo", [P, DC, GD], room, F32R)
        with ExitStack() as room:
            wo_hi = sb("wo_hi", [GD, REP, D], room, F32R)
            sb("room0_head", [P, HC * DC * P - 2 * HID - D - REP * D], room)
            down_sb = sb("down_sb", [STACK, HID + D], room)
        with ExitStack() as room:
            sb("room0_head_again", [P, HC * DC * P - 2 * HID - D], room)
            a_down_s = sb("a_down_s", [STACK, HID], room, F32R)
            b_down_s = sb("b_down_s", [STACK, D], room, F32R)
            down_part = sb("down_part", [STACK, HID], room, F32R)
        with ExitStack() as room:
            f3_hi = sb("f3_hi", [P, HC, DC, P], room, F32R)
        sb("room0", [P, HC * DC * P])
        with ExitStack() as room:
            y_t = sb("y_t", [P, DC, BLOCK], room)
            y_hi = sb("y_hi", [P, DC, BLOCK], room, F32R)
        with ExitStack() as room:
            v_wide = sb("v_wide", [P, BB, 2, G, HD], room)
        with ExitStack() as room:
            c_hi = sb("c_hi", [P, DC, BLOCK], room, F32R)
            c_lo = sb("c_lo", [P, DC, BLOCK], room, F32R)
        sb("room1", [P, 2 * DC * BLOCK])
        with ExitStack() as room:
            wq_sb = sb("wq_sb", [P, DC, REP, GD], room)
            k_all = sb("k_all", [GD, G, QG, S], room)
            v_all = sb("v_all", [P, N // P, GD], room)
        with ExitStack() as room:
            wq_lo = sb("wq_lo", [P, DC, REP, GD], room, F32R)
        with ExitStack() as room:
            f2_sb = sb("f2_sb", [P, HC, D], room)
        with ExitStack() as room:
            f2_lo = sb("f2_lo", [P, HC, D], room, F32R)
            c_odd = sb("c_odd", [P, BT, DC, S], room)
        sb("room2", [P, 3 * N])
        with ExitStack() as room:
            k_wide = sb("k_wide", [GD, 2, G, QG, S], room)
            q_t = sb("q_t", [GD, BB, REP, S], room)
        with ExitStack() as room:
            f2_hi_head = sb("f2_hi_head", [P, F2_HEAD, D], room, F32R)
            near = sb("near", [P, BB, P + 2], room)
        sb("room3", [P, F2_HEAD * D + BB * (P + 2)])
        with ExitStack() as room:
            params_sb = sb("params_sb", [P, sum(PARAMS.values())], room)
            hid0 = sb("hid0", [COND, B], room)
            hid1 = sb("hid1", [COND, B], room)
            att_wide = sb("att_wide", [B, BT, S], room)
            att_diag = sb("att_diag", [P, BT, B], room)
        with ExitStack() as room:
            wkq_hi = sb("wkq_hi", [P, DC, 1 + REP, GD], room, F32R)
        with ExitStack() as room:
            probs = sb("probs", [P, PROBS, 2, G, S], room)
            probs_t = sb("probs_t", [P, 2, 4, P], room)
        with ExitStack() as room:
            gate_hi = sb("gate_hi", [P, 2, BLOCK], room, F32R)
            gate_lo = sb("gate_lo", [P, 2, BLOCK], room, F32R)
            gate = sb("gate", [P, 2, BLOCK], room)
        sb("room4", [P, 6 * BLOCK])
        with ExitStack() as room:
            q_odd = sb("q_odd", [GD, BB, REP, S], room)
        with ExitStack() as room:
            ctx_hi = sb("ctx_hi", [GD, REP, 2 * P], room, F32R)
            ctx_lo = sb("ctx_lo", [GD, REP, 2 * P], room, F32R)
        with ExitStack() as room:
            f2_hi_tail = sb("f2_hi_tail", [P, HC - F2_HEAD, D], room, F32R)
            c_even = sb("c_even", [P, BT, DC, S], room)
        sb("room5", [P, REP * BLOCK])
        with ExitStack() as room:
            f1_sb = sb("f1_sb", [P, DC, HID], room)
            up_sb = sb("up_sb", [STACK, 2 * D + HID], room)
        with ExitStack() as room:
            f1_lo = sb("f1_lo", [P, DC, HID], room, F32R)
            a_up_s = sb("a_up_s", [STACK, 2, D], room, F32R)
            b_up_s = sb("b_up_s", [STACK, HID], room, F32R)
        sb("room6", [P, 4 * N])
        with ExitStack() as room:
            f3_sb = sb("f3_sb", [P, DC, HID], room)
        with ExitStack() as room:
            f3_lo = sb("f3_lo", [P, DC, HID], room, F32R)
        sb("room7", [P, DC * HID])
        with ExitStack() as room:
            x_sb = sb("x_sb", [P, TILES, D], room)
            y_lo = sb("y_lo", [P, DC, BLOCK], room, F32R)
            up_part = sb("up_part", [STACK, HID], room, F32R)
        with ExitStack() as room:
            sb("x_again", [P, TILES, D], room)
            wo_sb = sb("wo_sb", [GD, REP, D], room)
        with ExitStack() as room:
            sb("x_once_more", [P, TILES, D], room)
            wo_lo = sb("wo_lo", [GD, REP, D], room, F32R)
        with ExitStack() as room:
            f1_hi = sb("f1_hi", [P, DC, HID], room, F32R)
        sb("room8", [P, DC * HID])
        c_raw = (c_even, c_odd)
        a_part, b_part = up_part[2 * S:3 * S, 0:2 * D], up_part[S:2 * S, :]
        a_up, b_up = up_sb[:, 0:2 * D], up_sb[:, 2 * D:2 * D + HID]
        a_down, b_down = down_sb[:, 0:HID], down_sb[:, HID:HID + D]
        a_up_s_rows = a_up_s[:, :, :].rearrange("k f d -> k (f d)")
        q_stage = (q_t, q_odd)

        front = ps[0:2]
        score_bank = ps[2:4]
        turn_bank = ps[4:6]
        ctx_bank = ps[6:8]
        up_bank = ps[0:4]
        down_bank = ps[4:8]
        fold_bank = ps[4:8]

        x_rows = x.rearrange("(t p) d -> p t d", p=P)
        x1_rows = x1_dram.rearrange("(t p) d -> p t d", p=P)
        out_rows = out.rearrange("(t p) d -> p t d", p=P)
        x1_near = x1_dram.rearrange("(b s) (r n) -> r s b n", s=S, r=BT)

        mix_at = sum(PARAMS.values()) - S * S - S
        first = dict(zip(PARAMS, np.cumsum([0, *PARAMS.values()])))

        def param(name, rows=P):
            return params_sb[0:rows, int(first[name]):int(first[name]) + PARAMS[name]]

        f2_loads = [(f2_sb[:, 0:HC - 1, :], f2[0:(HC - 1) * P, :].rearrange("(c p) d -> p c d", p=P)),
                    (f2_sb[0:HW[-1], HC - 1, :], f2[(HC - 1) * P:HID, :])]

        def f2_hi(h):
            return (f2_hi_head[0:HW[h], h, :] if h < F2_HEAD else f2_hi_tail[0:HW[h], h - F2_HEAD, :])

        def split_parts(h):
            w, cols = HW[h], slice(h * P, h * P + HW[h])
            return ((f3_sb[:, :, cols], f3_hi[:, h, :, 0:w], f3_lo[:, :, cols]),
                    (f1_sb[:, :, cols], f1_hi[:, :, cols], f1_lo[:, :, cols]),
                    (f2_sb[0:w, h, :], f2_hi(h), f2_lo[0:w, h, :]))

        up_folds = [(f3_sb, c, 1) for c in range(DC)] + [(f1_sb, c, 0) for c in range(DC)]
        down_folds = (range(0, 4), range(4, HC - 4), (), range(HC - 4, HC))
        conv_order = [2, 3, 0, 1]

        def stack_copies(a, b, a_s, b_s, a_part, b_part):
            return ((a_part, a[2 * S:3 * S, :]), (b_part, b[S:2 * S, :]), (a_s[0:2 * S, :], a[0:2 * S, :]),
                    (b_s[0:S, :], b[0:S, :]), (b_s[2 * S:3 * S, :], b[2 * S:3 * S, :]))

        def pipeline(eng, step):
            for s in range(PAIRS):
                step(0, s, True, True)
            with eng.Fori(1, BLOCKS) as i:
                for s in range(PAIRS):
                    step(i, s, True, False)
            for s in range(PAIRS, PAIRS + OUT - 1):
                step(BLOCKS - 1, s, False, False)

        def emptied(use):
            return use // 2 + 1

        def blocks(eng, body):
            body(0, True, True)
            with eng.Fori(1, BLOCKS - 1) as i:
                body(i, False, True)
            body(BLOCKS - 1, False, False)

        block = ctx.enter_context(nc.Block())

        @block.sync
        def _(sp):
            sp.dma_start(params_sb[:, 0:mix_at], params[:, 0:mix_at]).then_inc(cond_loaded, 16)
            sp.dma_start(ident_sb[:, :], ident).then_inc(ident_loaded, 16)
            sp.dma_start(params_sb[:, mix_at:], params[:, mix_at:]).then_inc(mix_loaded, 16)
            sp.dma_start(up_sb[:, :], up_factors).then_inc(up_factors_loaded, 16)
            sp.dma_start(x_sb[:, :, :], x_rows[:, 0:TILES, :]).then_inc(x_loaded[0], 16)
            sp.dma_start(wv_sb[:, :, :], wv).then_inc(attn_loaded, 16)
            sp.wait_ge(shifts_act, 2)
            sp.dma_start(shifts_dram[1], mixb_sb[:, :]).then_inc(mix_shift_stored, 16)
            sp.wait_ge(mix_shift_stored, 16)
            mix_shifts = shifts_dram[1:2].rearrange("m b s -> m (b s)")
            sp.dma_start(mixb_all[:, 0:BLOCK], mix_shifts[:, 0:BLOCK].to_broadcast([P, BLOCK]))\
                .then_inc(mix_shift_spread[0], 16)
            sp.dma_start(mixb_all[:, BLOCK:N], mix_shifts[:, BLOCK:N].to_broadcast([P, N - BLOCK]))\
                .then_inc(mix_shift_spread[1], 16)
            sp.dma_start(rows[:, :, :], x_rows[:, TILES:2 * TILES, :]).then_inc(x_loaded[1], 16)
            sp.dma_start(shifts_dram[0], convb_sb[:, :]).then_inc(conv_shift_stored, 16)
            sp.dma_start(f3_sb[:, :, :], f3).then_inc(ffn_loaded, 16)
            sp.dma_start(f1_sb[:, :, :], f1).then_inc(ffn_loaded, 16)
            sp.wait_ge(conv_shift_stored, 16)
            sp.dma_start(convb_all[:, :], shifts_dram[0:1].rearrange("m b s -> m (b s)").to_broadcast([P, N]))\
                .then_inc(conv_shift_spread, 16)
            sp.dma_start(conv_sb[:, :, :], conv).then_inc(ffn_loaded, 16)
            sp.dma_start(bo_all[:, :], bo.to_broadcast([P, D])).then_inc(bo_spread, 16)
            sp.dma_start(causal_sb[:, :], causal).then_inc(causal_loaded, 16)

            def queries_and_keys(g):
                i, half = g // 2, g % 2
                if g >= 2:
                    sp.wait_ge(scores_ready, (i - 1) * PAIRS + (half + 1) * PAIRS // 2)
                sp.dma_start(q_t[:, half * HALF:(half + 1) * HALF, :, :],
                             q_dram[:, g * HALF:(g + 1) * HALF, :, :]).then_inc(q_loaded[half], 16)
                for k in range(G):
                    sp.dma_start(k_wide[k * HD:(k + 1) * HD, half, k, :, :],
                                 k_all[g * HD:(g + 1) * HD, k, :, :]).then_inc(k_loaded[half], 16)

            for i in range(BLOCKS):
                if i + 2 < BLOCKS:
                    sp.wait_ge(front_filled, i * USES + DC)
                    sp.dma_start((x_sb, rows)[i % 2][:, :, :], x_rows[:, (i + 2) * TILES:(i + 3) * TILES, :])\
                        .then_inc(x_loaded[i % 2], 16)
                if i == BLOCKS - 1:
                    sp.wait_ge(front_emptied[1], i * (USES // 2) + emptied(DC + 1) + 1)
                    sp.wait_ge(q_stored[0], 16 * BLOCKS // 2)
                    sp.wait_ge(zeros_set, 4)
                    for g in range(2):
                        queries_and_keys(g)
                if i == BLOCKS - 2:
                    sp.wait_ge(front_filled, i * USES + DC)
                    sp.dma_start(x_sb[:, :, :], x_rows[:, 0:TILES, :]).then_inc(x_reloaded, 16)
                for n in (DC + REP, DC + REP + 1):
                    sp.wait_ge(front_emptied[n % 2], i * (USES // 2) + emptied(n) + 1)
                if i == BLOCKS - 1:
                    sp.wait_ge(front_filled, PROJECTED)
                    sp.dma_start(wo_sb[:, :, :], wo).then_inc(wo_loaded, 16)
                if i >= 1:
                    sp.wait_ge(q_stored[(i - 1) % 2], 16 * ((i + 1) // 2))
                sp.dma_start(q_dram[:, i * BB:(i + 1) * BB, :, :], q_stage[i % 2][:, :, :, :])\
                    .then_inc(q_stored[i % 2], 16)

            def load_near(i):
                for r in range(BT):
                    sp.dma_start(near[r * S:(r + 1) * S, :, 1:P + 1],
                                 x1_near[r, :, bass.ds(i * BB, BB), :]).then_inc(near_loaded, 16)

            def store_x1(i, t):
                sp.wait_ge(front_emptied[t % 2], emptied(PROJECTED + i * TILES + t) + 1)
                sp.dma_start(x1_rows[:, i * TILES + t, :], rows[:, t, :]).then_inc(x1_stored[t], 16)

            sp.wait_ge(front_emptied[0], emptied(PROJECTED))
            sp.wait_ge(front_emptied[1], emptied(PROJECTED))
            sp.dma_start(down_sb[:, :], down_factors).then_inc(down_factors_loaded, 16)
            sp.wait_ge(q_stored[1], 16 * BLOCKS // 2)
            for i in range(BLOCKS):
                if i + 1 < BLOCKS:
                    queries_and_keys(2 * i + 2)
                    store_x1(i, 0)
                    queries_and_keys(2 * i + 3)
                    sp.wait_ge(resid_ready, (i + 1) * TILES)
                    sp.dma_start(x_sb[:, :, :], x_rows[:, (i + 1) * TILES:(i + 2) * TILES, :])\
                        .then_inc(x_reloaded, 16)
                else:
                    for n in range(2):
                        sp.wait_ge(k_loaded[n], 16 * G * BLOCKS)
                    sp.wait_ge(v_spread, 4 * BT * BLOCKS)
                    for dst, src in f2_loads:
                        sp.dma_start(dst, src).then_inc(f2_loaded, 16)
                    for stored in x1_stored:
                        sp.wait_ge(stored, 16 * i)
                    store_x1(i, 0)
                    sp.wait_ge(scores_ready, BLOCKS * PAIRS)
                    load_near(0)
                for t in range(1, TILES):
                    store_x1(i, t)

            def load_rows(i):
                sp.dma_start(rows[:, :, :], x1_rows[:, bass.ds(i * TILES, TILES), :]).then_inc(x1_loaded, 16)

            def store_out(i):
                for t in range(TILES):
                    sp.wait_ge(out_ready, i * TILES + t + 1)
                    sp.dma_start(out_rows[:, bass.ds(i * TILES + t, 1), :],
                                 rows[:, t:t + 1, :]).then_inc(out_stored, 16)

            for stored in x1_stored:
                sp.wait_ge(stored, 16 * BLOCKS)
            load_rows(0)
            with sp.Fori(0, BLOCKS - 1) as i:
                sp.wait_ge(conv_filled, (i + 1) * BT)
                load_near(i + 1)
                store_out(i)
                sp.wait_ge(out_stored, (i + 1) * TILES * 16)
                load_rows(i + 1)
            store_out(BLOCKS - 1)
            sp.wait_ge(out_stored, 16 * TILES * BLOCKS)

        @block.gpsimd
        def _(pool):
            pool.memset(ones[:, :], 1.0).then_inc(ones_set, 1)
            pool.memset(att_wide[:, :, :], 0.0).then_inc(zeros_set, 1)
            pool.memset(att_diag[:, :, :], 0.0).then_inc(zeros_set, 1)
            pool.memset(mix[:, :, :, :], 0.0).then_inc(zeros_set, 1)
            pool.memset(k_wide[:, :, :, :, :], 0.0).then_inc(zeros_set, 1)
            pool.wait_ge(wkq_hi_split, 1)
            pool.tensor_tensor(wk_lo[:, :, :], wk_sb[:, :, :], wkq_hi[:, :, 0, :].bitcast(F32), ALU.subtract)\
                .then_inc(wkq_lo_split, 1)
            for j in range(REP):
                pool.wait_ge(wkq_hi_split, j + 2)
                pool.tensor_tensor(wq_lo[:, :, j, :], wq_sb[:, :, j, :], wkq_hi[:, :, 1 + j, :].bitcast(F32),
                                   ALU.subtract).then_inc(wkq_lo_split, 1)
            pool.wait_ge(wkq_lo_split, 1 + REP)
            pool.wait_ge(zeros_set, 4)
            pool.wait_ge(up_stacked, 2)
            pool.tensor_tensor(a_up_s_rows[2 * S:3 * S, :], a_up[2 * S:3 * S, :], a_part.bitcast(F32),
                               ALU.subtract).then_inc(up_lo_stacked, 1)
            pool.wait_ge(up_lo_stacked, 1)
            pool.tensor_tensor(b_up_s[S:2 * S, :], b_up[S:2 * S, :], b_part.bitcast(F32),
                               ALU.subtract).then_inc(up_lo_stacked, 1)
            pool.wait_ge(up_lo_stacked, 2)
            pool.wait_ge(y_lo_ready, DC * BLOCKS)
            for half in range(2):
                pool.wait_ge(front_filled, PROJECTED - (1 - half) * (1 + REP))
                pool.memset(v_wide[:, half * HALF:(half + 1) * HALF, :, :, :], 0.0).then_inc(v_cleared, 1)
            pool.wait_ge(bo_spread, 16)

            def step(i, s, start, first):
                n = i * PAIRS + s
                if start:
                    pool.wait_ge(top_ready, n + 1)
                    pr = probs[:, s % PROBS].rearrange("p b g k -> p (b g) k")
                    pool.tensor_tensor(pr, pr, top[:, s % PROBS].unsqueeze(2).to_broadcast([P, 2 * G, S]),
                                       ALU.subtract).then_inc(shifted, 1)
                if (s >= 1 or not first) and s < PAIRS + 1:
                    pool.wait_ge(inv_ready, n)
                    pr = probs[:, (s - 1) % PROBS].rearrange("p b g k -> p (b g) k")
                    pool.tensor_tensor(pr, pr, inv[:, (s - 1) % PROBS].unsqueeze(2).to_broadcast([P, 2 * G, S]),
                                       ALU.mult).then_inc(probs_ready, 1)
                if start and s % 2:
                    t = s // 2
                    if t == 0:
                        pool.wait_ge(x_reloaded, (i + 1) * 16)
                    if not first:
                        pool.wait_ge(x1_stored[t], i * 16)
                    pool.tensor_tensor(rows[:, t, :].rearrange("p (r n) -> p r n", r=BT),
                                       x_sb[:, t, :].rearrange("p (n r) -> p r n", r=BT),
                                       bo_all[:, :].rearrange("p (r n) -> p r n", r=BT), ALU.add)\
                        .then_inc(resid_ready, 1)
                if s == PAIRS:
                    pool.wait_ge(scores_ready, BLOCKS * PAIRS)
                    pool.memset(near[:, :, 0:1], 0.0).then_inc(near_zeroed, 1)
                    pool.memset(near[:, :, P + 1:P + 2], 0.0).then_inc(near_zeroed, 1)

            pipeline(pool, step)
            for h in range(HC):
                for n, (w, hi, lo) in enumerate(split_parts(h)):
                    pool.wait_ge(hi_split, 3 * h + n + 1)
                    pool.tensor_tensor(lo, w, hi.bitcast(F32), ALU.subtract).then_inc(lo_split, 1)

        @block.scalar
        def _(act):
            act.wait_ge(ones_set, 1)
            act.activation(neg_top[0:1, :], ones[0:1, 0:1], ACT.Gelu).then_inc(warmed, 1)
            act.wait_ge(cond_loaded, 16)
            act.dma_start(wk_sb[:, :, :], wk).then_inc(attn_loaded, 16)
            act.dma_start(wq_sb[:, :, :, :], wq).then_inc(attn_loaded, 16)
            act.wait_ge(cond_pe, 1)
            act.activation(hid0[:, :], ps[0][:, 0:B], ACT.Gelu, bias=param("b0")).then_inc(cond_act, 1)
            act.wait_ge(cond_pe, 2)
            act.activation(hid1[:, :], ps[1][:, 0:B], ACT.Gelu, bias=param("b1")).then_inc(cond_act, 1)
            act.wait_ge(shifts_pe, 1)
            act.copy(convb_sb[:, :], ps[5][0:B, 0:S]).then_inc(shifts_act, 1)
            act.wait_ge(cond_dve, 1)
            act.activation(att[:, :], ps[2][0:B, 0:K], ACT.Exp, bias=neg_top[:, 0:1],
                           accum_out=att_sum[:, 0:1]).then_inc(cond_act, 1)
            act.wait_ge(shifts_pe, 2)
            act.copy(mixb_sb[:, :], ps[6][0:B, 0:S]).then_inc(shifts_act, 1)
            act.wait_ge(up_factors_loaded, 16)
            for copied, src in stack_copies(a_up, b_up, a_up_s_rows, b_up_s, a_part, b_part):
                act.copy(copied, src).then_inc(up_stacked, 1)
            act.wait_ge(cond_pe, 8)
            act.wait_ge(attn_loaded, 16 * 3)
            act.copy(wkq_hi[:, :, 0, :], wk_sb[:, :, :]).then_inc(wkq_hi_split, 1)
            for j in range(REP):
                act.copy(wkq_hi[:, :, 1 + j, :], wq_sb[:, :, j, :]).then_inc(wkq_hi_split, 1)
            with act.Fori(0, BLOCKS // 2) as i:
                for half in range(2):
                    blk = 2 * i + half
                    for c in range(DC):
                        act.wait_ge(front_emptied[c % 2], blk * (USES // 2) + emptied(c) + 1)
                        act.copy(y_hi[:, c, :], y_t[:, c, :]).then_inc(y_hi_ready, 1)
                    n = DC
                    act.wait_ge(front_filled, blk * USES + n + 1)
                    act.copy(v_all[:, bass.ds(blk * TILES, TILES), :],
                             front[n % 2][:, :].rearrange("p (t c) -> p t c", t=TILES))\
                        .then_inc(front_emptied[n % 2], 1)
                    n = DC + 1
                    act.wait_ge(front_filled, blk * USES + n + 1)
                    act.copy(k_all[:, :, bass.ds(blk * 2, 2), :].rearrange("p g c s -> p c g s"),
                             front[n % 2][:, :].rearrange("p (c g s) -> p c g s", c=2, s=S))\
                        .then_inc(front_emptied[n % 2], 1)
                    if half == 1:
                        act.wait_ge(q_stored[0], 16 * (i + 1))
                    for j in range(REP):
                        n = DC + 2 + j
                        act.wait_ge(front_filled, blk * USES + n + 1)
                        act.copy(q_stage[half][:, :, j, :],
                                 front[n % 2][:, :].rearrange("p (b s) -> p b s", s=S))\
                            .then_inc(front_emptied[n % 2], 1)

            copies = stack_copies(a_down, b_down, a_down_s, b_down_s, down_part[2 * S:3 * S, :],
                                  down_part[S:2 * S, 0:D])

            def step(i, s, start, first):
                n = i * PAIRS + s
                if first and s == 3:
                    act.wait_ge(wo_loaded, 16)
                if first and 3 <= s < 5:
                    for j in (2 * s - 6, 2 * s - 5):
                        act.copy(wo_hi[:, j, :], wo_sb[:, j, :]).then_inc(wo_hi_split, 1)
                if s >= PAIRS:
                    act.wait_ge(down_factors_loaded, 16)
                    act.copy(*copies[s - PAIRS]).then_inc(down_stacked, 1)
                if (s >= TURN or not first) and s - TURN < PAIRS:
                    act.wait_ge(turned, n - TURN + 1)
                    act.copy(probs_t[:, (s - TURN) % 2], turn_bank[(s - TURN) % 2][:, :]
                             .rearrange("p (c q) -> p c q", q=P)).then_inc(turned_copied, 1)
                if (s >= CONTEXT or not first) and s - CONTEXT < PAIRS:
                    q = (s - CONTEXT) % PAIRS
                    act.wait_ge(ctx_filled, n - CONTEXT + 1)
                    if first and s == CONTEXT:
                        act.wait_ge(q_stored[1], 16 * BLOCKS // 2)
                    if s - CONTEXT >= 4 or not first:
                        act.wait_ge(front_filled, PROJECTED + i * TILES + (s - CONTEXT) // 2 - 1)
                    act.copy(ctx_hi[:, :, q % 4 * 2 * S:(q % 4 + 1) * 2 * S].rearrange("p j (b s) -> p b j s", s=S),
                             ctx_bank[q % 2][:, 0:2 * P].rearrange("p (b j s) -> p b j s", b=2, j=REP))\
                        .then_inc(ctx_copied, 1)
                if start:
                    act.wait_ge(shifted, n + 1)
                    act.activation(probs[:, s % PROBS], probs[:, s % PROBS], ACT.Exp, scale=SCALE)\
                        .then_inc(exp_ready, 1)

            pipeline(act, step)

            def split(h, parts=(0, 1, 2)):
                for n in parts:
                    w, hi, _ = split_parts(h)[n]
                    if n == 2:
                        act.wait_ge(down_folded, h + 1)
                    act.copy(hi, w).then_inc(hi_split, 1)

            def round_conv(i):
                for n, q in enumerate(conv_order):
                    act.wait_ge(c_ready, i * BT + n + 1)
                    act.copy(c_hi[:, :, q * P:(q + 1) * P].rearrange("p s (b o) -> p b s o", o=S),
                             c_raw[n % 2][:, :, :, :]).then_inc(c_hi_ready, 1)

            def block_of_rows(i, first, more):
                for h, w in enumerate(HW):
                    act.wait_ge(up1_filled, i * HC + h + 1)
                    if h >= 2 or not first:
                        act.wait_ge(gate_lo_ready, i * HC + max(h - 1, 0))
                    act.activation(gate[0:w, h % 2, :], up_bank[2 * (h % 2)][0:w, :], ACT.Silu)\
                        .then_inc(silu_ready, 1)
                    act.wait_ge(gate_ready, i * HC + h + 1)
                    act.copy(gate_hi[0:w, h % 2, :], gate[0:w, h % 2, :]).then_inc(gate_hi_ready, 1)
                    if first and h + 2 < HC:
                        split(h + 2)
                if more:
                    round_conv(i + 1)

            act.wait_ge(up_folded, FOLDS)
            act.wait_ge(scores_ready, BLOCKS * PAIRS)
            act.wait_ge(front_filled, PROJECTED + BLOCKS * TILES)
            split(0, (0, 1))
            round_conv(0)
            split(0, (2,))
            split(1)
            blocks(act, block_of_rows)

        @block.vector
        def _(dve):
            dve.wait_ge(warmed, 1)
            dve.wait_ge(cond_pe, 3)
            dve.tensor_reduce(neg_top[:, :], ps[2][0:B, 0:K], AX_X, ALU.max, negate=True).then_inc(cond_dve, 1)
            dve.wait_ge(cond_act, 3)
            dve.reciprocal(att_inv[:, :], att_sum[:, :]).then_inc(cond_dve, 1)
            dve.wait_ge(cond_dve, 2)
            dve.wait_ge(zeros_set, 2)
            dve.tensor_scalar(att_wide[:, :, 0:K], att[:, :].unsqueeze(1).to_broadcast([B, BT, K]), att_inv[:, 0:1],
                              None, ALU.mult).then_inc(cond_dve, 1)
            dve.wait_ge(cond_pe, 4)
            for c in range(BT):
                dve.tensor_copy(att_diag[c * S:c * S + K, c, :], ps[3][c * S:c * S + K, 0:B]).then_inc(cond_dve, 1)
            dve.wait_ge(zeros_set, 3)
            for n in range(4):
                dve.wait_ge(cond_pe, 5 + n)
                made = ps[n][:, :].rearrange("p (o t c) -> p t o c", o=8, c=BT)
                for c in range(BT):
                    copy = dve.tensor_copy(mix[c * S:(c + 1) * S, :, c, n * 8:(n + 1) * 8],
                                           made[c * S:(c + 1) * S, :, :, c])
                copy.then_inc(front_emptied[n] if n < 2 else mix_made, 1)
            with dve.Fori(0, BLOCKS // 2) as i:
                for half in range(2):
                    dve.wait_ge(mix_shift_spread[half], 16)
                    blk = 2 * i + half
                    for c in range(DC):
                        dve.wait_ge(front_filled, blk * USES + c + 1)
                        dve.tensor_tensor(y_t[:, c, :], front[c % 2][:, :],
                                          mixb_all[:, bass.ds(blk * BLOCK, BLOCK)], ALU.add)\
                            .then_inc(front_emptied[c % 2], 1)
                    for c in range(DC):
                        dve.wait_ge(y_hi_ready, blk * DC + c + 1)
                        dve.tensor_tensor(y_lo[:, c, :], y_t[:, c, :], y_hi[:, c, :].bitcast(F32), ALU.subtract)\
                            .then_inc(y_lo_ready, 1)
                for n, (f, c, _) in enumerate(2 * up_folds):
                    dst = f[:, c, bass.ds((2 * i + n // len(up_folds)) * FOLD_N, FOLD_N)]
                    dve.wait_ge(up_fold_filled, i * (FOLDS // 2) + n + 1)
                    dve.scalar_tensor_tensor(out=dst, in0=fold_bank[n % 4][:, 0:FOLD_N], scalar=LORA_SCALE,
                                             in1=dst, op0=ALU.mult, op1=ALU.add).then_inc(up_folded, 1)
            dve.wait_ge(causal_loaded, 16)
            dve.wait_ge(front_emptied[0], emptied(PROJECTED))

            def spread_values(i, half):
                vg = v_all[:, :, :].rearrange("p (c h) (g d) -> p c h g d", h=2, d=HD)
                vw = v_wide[:, half * HALF:(half + 1) * HALF, :, :, :].rearrange("p c h (z g) d -> p c h z g d", z=2)
                for g in range(BT):
                    for h in range(2):
                        dve.tensor_copy(vw[g * S:(g + 1) * S, :, h, h, g, :],
                                        vg[g * S:(g + 1) * S, :, h, bass.ds(2 * i + half, 1), :]
                                        .rearrange("p c g d -> p c (g d)")).then_inc(v_spread, 1)

            def step(i, s, start, first):
                n = i * PAIRS + s
                if start:
                    pr = probs[:, s % PROBS].rearrange("p b g k -> p (b g) k")
                    dve.wait_ge(scores_ready, n + 1)
                    if s >= PROBS or not first:
                        dve.wait_ge(turned, n - PROBS + 1)
                    dve.tensor_tensor(pr, score_bank[s % 2][:, :].rearrange("p (c k) -> p c k", k=S),
                                      causal_sb[:, :].unsqueeze(1).to_broadcast([P, 2 * G, S]), ALU.add)\
                        .then_inc(masked, 1)
                    dve.wait_ge(masked, n + 1)
                    dve.tensor_reduce(top[:, s % PROBS, :], pr, AX_X, ALU.max).then_inc(top_ready, 1)
                if (s >= 1 or not first) and s < PAIRS + 1:
                    q = (s - 1) % PROBS
                    dve.wait_ge(exp_ready, n)
                    dve.tensor_reduce(total[:, q, :], probs[:, q].rearrange("p b g k -> p (b g) k"),
                                      AX_X, ALU.add).then_inc(sum_ready, 1)
                    dve.wait_ge(sum_ready, n)
                    dve.reciprocal(inv[:, q, :], total[:, q, :]).then_inc(inv_ready, 1)
                if start and s == 0:
                    if first:
                        dve.wait_ge(v_cleared, 1)
                    else:
                        dve.wait_ge(ctx_filled, i * PAIRS - PAIRS // 2)
                    spread_values(i, 0)
                if start and s == CONTEXT:
                    if first:
                        dve.wait_ge(v_cleared, 2)
                    else:
                        dve.wait_ge(ctx_filled, i * PAIRS)
                    spread_values(i, 1)
                if (s >= CONTEXT or not first) and s - CONTEXT < PAIRS:
                    q = (s - CONTEXT) % PAIRS
                    there = slice(q % 4 * 2 * S, (q % 4 + 1) * 2 * S)
                    dve.wait_ge(ctx_copied, n - CONTEXT + 1)
                    dve.tensor_tensor(ctx_lo[:, :, there].rearrange("p j (b s) -> p b j s", s=S),
                                      ctx_bank[q % 2][:, 0:2 * P].rearrange("p (b j s) -> p b j s", b=2, j=REP),
                                      ctx_hi[:, :, there].rearrange("p j (b s) -> p b j s", s=S).bitcast(F32),
                                      ALU.subtract).then_inc(ctx_lo_ready, 1)
                if first and 4 <= s < 6:
                    for j in (2 * s - 8, 2 * s - 7):
                        dve.wait_ge(wo_hi_split, j + 1)
                        dve.tensor_tensor(wo_lo[:, j, :], wo_sb[:, j, :], wo_hi[:, j, :].bitcast(F32), ALU.subtract)\
                            .then_inc(wo_lo_split, 1)
                if s == PAIRS + OUT - 2:
                    dve.wait_ge(down_stacked, 2)
                    dve.tensor_tensor(a_down_s[2 * S:3 * S, :], a_down[2 * S:3 * S, :],
                                      down_part[2 * S:3 * S, :].bitcast(F32), ALU.subtract).then_inc(down_lo_stacked, 1)
                    dve.tensor_tensor(b_down_s[S:2 * S, :], b_down[S:2 * S, :],
                                      down_part[S:2 * S, 0:D].bitcast(F32), ALU.subtract).then_inc(down_lo_stacked, 1)
                if s % 2 == 0 and (s >= OUT or not first):
                    t = (s - OUT) // 2 % TILES
                    tile = i * TILES + (s - OUT) // 2
                    dve.wait_ge(front_filled, PROJECTED + tile + 1)
                    dve.wait_ge(resid_ready, tile + 1)
                    dve.tensor_tensor(rows[:, t, :], front[t % 2][:, :], rows[:, t, :], ALU.add)\
                        .then_inc(front_emptied[t % 2], 1)

            pipeline(dve, step)

            def fold_down(h):
                dst = f2_sb[0:HW[h], h, :]
                dve.wait_ge(down_fold_filled, h + 1)
                dve.scalar_tensor_tensor(out=dst, in0=fold_bank[h % 4][0:HW[h], :], scalar=LORA_SCALE,
                                         in1=dst, op0=ALU.mult, op1=ALU.add).then_inc(down_folded, 1)

            def conv_lo(i, n):
                q = conv_order[n]
                dve.wait_ge(c_hi_ready, i * BT + n + 1)
                dve.tensor_tensor(c_lo[:, :, q * P:(q + 1) * P].rearrange("p s (b o) -> p b s o", o=S),
                                  c_raw[n % 2][:, :, :, :],
                                  c_hi[:, :, q * P:(q + 1) * P].rearrange("p s (b o) -> p b s o", o=S).bitcast(F32),
                                  ALU.subtract).then_inc(c_lo_ready, 1)

            def copy_conv(i, first=False):
                for n, q in enumerate(conv_order):
                    dve.wait_ge(conv_filled, i * BT + n + 1)
                    if n >= 2:
                        dve.wait_ge(c_lo_ready, i * BT + n - 1)
                    cb = convb_all[:, bass.ds(i * BLOCK + q * P, P)].rearrange("p (b o) -> p b o", o=S)
                    dve.tensor_tensor(c_raw[n % 2][:, :, :, :],
                                      up_bank[q][:, :].rearrange("p (b s o) -> p b s o", s=DC, o=S),
                                      cb.unsqueeze(2).to_broadcast([P, BT, DC, S]), ALU.add)\
                        .then_inc(c_ready, 1)
                    if n:
                        conv_lo(i, n - 1)
                    if n == BT - 1:
                        conv_lo(i, n)
                    if first:
                        for h in down_folds[n]:
                            fold_down(h)

            def block_of_rows(i, first, more):
                for h, w in enumerate(HW):
                    dve.wait_ge(up3_filled, i * HC + h + 1)
                    dve.wait_ge(silu_ready, i * HC + h + 1)
                    dve.tensor_tensor(gate[0:w, h % 2, :], up_bank[2 * (h % 2) + 1][0:w, :], gate[0:w, h % 2, :],
                                      ALU.mult).then_inc(gate_ready, 1)
                    dve.wait_ge(gate_hi_ready, i * HC + h + 1)
                    dve.tensor_tensor(gate_lo[0:w, h % 2, :], gate[0:w, h % 2, :],
                                      gate_hi[0:w, h % 2, :].bitcast(F32), ALU.subtract).then_inc(gate_lo_ready, 1)
                if more:
                    copy_conv(i + 1)
                dve.wait_ge(x1_loaded, 16 * (i + 1))
                for t in range(TILES):
                    dve.wait_ge(down_filled, i * TILES + t + 1)
                    dve.tensor_tensor(rows[:, t, :], down_bank[t][:, :], rows[:, t, :], ALU.add)\
                        .then_inc(out_ready, 1)

            dve.wait_ge(conv_shift_spread, 16)
            dve.wait_ge(ctx_filled, BLOCKS * PAIRS)
            dve.wait_ge(front_filled, PROJECTED + BLOCKS * TILES)
            copy_conv(0, first=True)
            blocks(dve, block_of_rows)

        @block.tensor
        def _(pe):
            pe.wait_ge(cond_loaded, 16)
            pe.matmul(ps[0][:, 0:B], param("w0"), param("cond_t"), start=True, stop=True).then_inc(cond_pe, 1)
            pe.wait_ge(ones_set, 1)
            pe.matmul(ps[5][0:B, 0:S], param("cond_t"), param("conv_cond"), start=True, stop=False)
            pe.matmul(ps[5][0:B, 0:S], ones[:, :], param("conv_bias", 1), start=False, stop=True)\
                .then_inc(shifts_pe, 1)
            pe.wait_ge(cond_act, 1)
            pe.matmul(ps[1][:, 0:B], param("w1"), hid0[:, :], start=True, stop=True).then_inc(cond_pe, 1)
            pe.wait_ge(cond_act, 2)
            pe.matmul(ps[2][0:B, 0:K], hid1[:, :], param("w2"), start=True, stop=False)
            pe.matmul(ps[2][0:B, 0:K], ones[:, :], param("b2", 1), start=False, stop=True).then_inc(cond_pe, 1)
            pe.wait_ge(cond_dve, 3)
            pe.wait_ge(ident_loaded, 16)
            pe.transpose(ps[3][:, 0:B], att_wide[:, :, :].rearrange("b c k -> b (c k)"), ident_sb[0:B, 0:B])\
                .then_inc(cond_pe, 1)
            pe.wait_ge(cond_dve, 3 + BT)
            pe.wait_ge(mix_loaded, 16)
            pe.matmul(ps[6][0:B, 0:S], att_diag[0:K, 0, :], param("mix_b", K), start=True, stop=True)\
                .then_inc(shifts_pe, 1)
            for m in range(S // BT):
                mm = pe.matmul(ps[m // 2][:, m % 2 * BT * B:(m % 2 + 1) * BT * B],
                               param("mix_w")[:, m * P:(m + 1) * P],
                               att_diag[:, :, :].rearrange("k o b -> k (o b)"), start=True, stop=True)
                if m % 2:
                    mm.then_inc(cond_pe, 1)
            pe.wait_ge(front_emptied[0], emptied(0))
            pe.wait_ge(front_emptied[1], emptied(1))
            pe.wait_ge(mix_made, 2)
            pe.wait_ge(attn_loaded, 16 * 3)

            def fold_up(i, m):
                if m == 0:
                    pe.wait_ge(up_stacked, 5)
                    pe.wait_ge(up_lo_stacked, 2)
                    pe.wait_ge(ffn_loaded, 16 * 3)
                if m >= 4:
                    pe.wait_ge(up_folded, i * (FOLDS // 2) + m - 3)
                _, c, factor = up_folds[m % len(up_folds)]
                pe.matmul(fold_bank[m % 4][:, 0:FOLD_N], a_up_s[:, factor, c * P:(c + 1) * P],
                          b_up_s[:, bass.ds((2 * i + m // len(up_folds)) * FOLD_N, FOLD_N)],
                          start=True, stop=True).then_inc(up_fold_filled, 1)

            with pe.Fori(0, BLOCKS // 2) as i:
                for half, buf in enumerate((x_sb, rows)):
                    blk = 2 * i + half

                    def bank_free(n):
                        pe.wait_ge(front_emptied[n % 2], blk * (USES // 2) + emptied(n))

                    pe.wait_ge(x_loaded[half], 16 * (i + 1))
                    for c in range(DC):
                        bank_free(c)
                        for t in range(TILES):
                            mm = pe.matmul(front[c % 2][:, t * P:(t + 1) * P], buf[:, t, c * P:(c + 1) * P],
                                           mix[:, bass.ds(blk * TILES + t, 1), :, :]
                                           .rearrange("p t c o -> p (t c o)"), start=True, stop=True)
                        mm.then_inc(front_filled, 1)
                    bank_free(DC)
                    for c in range(DC):
                        if c % 2:
                            bank_free(c + 2)
                        for t in range(TILES):
                            mm = pe.matmul(front[DC % 2][:, t * P:(t + 1) * P], y_t[:, c, t * P:(t + 1) * P],
                                           wv_sb[:, c, :], start=(c == 0 and t == 0),
                                           stop=(c == DC - 1 and t == TILES - 1))
                    mm.then_inc(front_filled, 1)
                    pe.wait_ge(y_lo_ready, (blk + 1) * DC)
                    for j in range(1 + REP):
                        n = DC + 1 + j
                        bank_free(n)
                        pe.wait_ge(wkq_lo_split, j + 1)
                        w_hi, w_lo = wkq_hi[:, :, j, :], wk_lo[:, :, :] if j == 0 else wq_lo[:, :, j - 1, :]
                        for m, (w, y) in enumerate(((w_hi, y_hi), (w_hi, y_lo), (w_lo, y_hi))):
                            for c in range(DC):
                                mm = pe.matmul(front[n % 2][:, :], w[:, c, :], y[:, c, :],
                                               start=(m == 0 and c == 0), stop=(m == 2 and c == DC - 1))
                        mm.then_inc(front_filled, 1)
                        if half == 1 and j < REP:
                            for m in range(j * 4, (j + 1) * 4):
                                fold_up(i, m)
                pe.wait_ge(up_folded, (i + 1) * (FOLDS // 2))

            def step(i, s, start, first):
                n = i * PAIRS + s
                if start:
                    if s % (PAIRS // 2) == 0:
                        half = s // (PAIRS // 2)
                        pe.wait_ge(q_loaded[half], (i + 1) * 16)
                        pe.wait_ge(k_loaded[half], (i + 1) * G * 16)
                    if s >= 2 or not first:
                        pe.wait_ge(masked, n - 1)
                    for b in range(2):
                        c = 2 * s + b
                        mm = pe.matmul(score_bank[s % 2][:, b * G * S:(b + 1) * G * S],
                                       q_t[:, c, :, :].rearrange("p j s -> p (j s)"),
                                       k_wide[:, c // HALF, :, c % HALF, :], start=True, stop=True)
                    mm.then_inc(scores_ready, 1)
                if (s >= TURN or not first) and s - TURN < PAIRS:
                    q = s - TURN
                    pe.wait_ge(probs_ready, n - TURN + 1)
                    if q >= 2 or not first:
                        pe.wait_ge(turned_copied, n - TURN - 1)
                    for b in range(2):
                        for h in range(2):
                            mm = pe.transpose(turn_bank[q % 2][:, (2 * b + h) * P:(2 * b + h + 1) * P],
                                              probs[:, q % PROBS, b, 4 * h:4 * h + 4, :].rearrange("p g k -> p (g k)"),
                                              ident_sb[:, :])
                    mm.then_inc(turned, 1)
                if (s >= CONTEXT or not first) and s - CONTEXT < PAIRS:
                    q = (s - CONTEXT) % PAIRS
                    if q % (PAIRS // 2) == 0:
                        half = (s - CONTEXT) // (PAIRS // 2)
                        pe.wait_ge(v_spread, (2 * i + half + 1) * 2 * BT)
                    pe.wait_ge(turned_copied, n - CONTEXT + 1)
                    if s - CONTEXT >= 2 or not first:
                        pe.wait_ge(ctx_lo_ready, n - CONTEXT - 1)
                    for b in range(2):
                        for h in range(2):
                            mm = pe.matmul(ctx_bank[q % 2][:, b * P:(b + 1) * P],
                                           v_wide[:, 2 * q + b, h].rearrange("p g d -> p (g d)"),
                                           probs_t[:, q % 2, 2 * b + h, :], start=(h == 0), stop=(h == 1))
                    mm.then_inc(ctx_filled, 1)
                if first and s == OUT:
                    pe.wait_ge(wo_lo_split, REP)
                if s % 2 == 0 and (s >= OUT or not first):
                    t = (s - OUT) // 2 % TILES
                    tile = i * TILES + (s - OUT) // 2
                    pe.wait_ge(ctx_lo_ready, n - OUT + 2)
                    pe.wait_ge(front_emptied[t % 2], emptied(PROJECTED) + i * (TILES // 2) + (s - OUT) // 2 // 2)
                    for m, (c_part, w) in enumerate(((ctx_hi, wo_hi), (ctx_hi, wo_lo), (ctx_lo, wo_hi))):
                        for j in range(REP):
                            mm = pe.matmul(front[t % 2][:, :], c_part[:, j, t % 2 * P:(t % 2 + 1) * P], w[:, j, :],
                                           start=(m == 0 and j == 0), stop=(m == 2 and j == REP - 1))
                    mm.then_inc(front_filled, 1)

            pipeline(pe, step)

            def convolve(i, first=False):
                pe.wait_ge(near_loaded, 16 * BT * (i + 1))
                for n, q in enumerate(conv_order):
                    if not first:
                        pe.wait_ge(gate_ready, i * HC - (1 if q >= 2 else 0))
                    elif q < 2:
                        pe.wait_ge(front_emptied[q], emptied(PROJECTED + BLOCKS * TILES))
                    for b in range(BT):
                        for m in range(NEAR):
                            mm = pe.matmul(up_bank[q][:, b * P:(b + 1) * P], near[:, q * BT + b, m:m + P],
                                           conv_sb[:, m, :], start=(m == 0), stop=(m == NEAR - 1))
                    mm.then_inc(conv_filled, 1)
                    if first:
                        for h in down_folds[n]:
                            fold_down(h)

            def fold_down(h):
                if h >= 4:
                    pe.wait_ge(down_folded, h - 3)
                pe.matmul(fold_bank[h % 4][0:HW[h], :], a_down_s[:, h * P:h * P + HW[h]], b_down_s[:, :],
                          start=True, stop=True).then_inc(down_fold_filled, 1)

            def up(i, h, first):
                w, cols = HW[h], slice(h * P, h * P + HW[h])
                if first:
                    pe.wait_ge(lo_split, 3 * h + 2)
                if h >= 2:
                    pe.wait_ge(gate_ready, i * HC + h - 1)
                for parts, bank, filled in (
                        (((f1_hi[:, :, cols], c_hi), (f1_hi[:, :, cols], c_lo), (f1_lo[:, :, cols], c_hi)),
                         up_bank[2 * (h % 2)], up1_filled),
                        (((f3_hi[:, h, :, 0:w], c_hi), (f3_hi[:, h, :, 0:w], c_lo), (f3_lo[:, :, cols], c_hi)),
                         up_bank[2 * (h % 2) + 1], up3_filled)):
                    for n, (f, c_part) in enumerate(parts):
                        for c in range(DC):
                            mm = pe.matmul(bank[0:w, :], f[:, c, :], c_part[:, c, :],
                                           start=(n == 0 and c == 0), stop=(n == 2 and c == DC - 1))
                    mm.then_inc(filled, 1)

            def down(i, h, first):
                w = HW[h]
                if first:
                    pe.wait_ge(lo_split, 3 * h + 3)
                pe.wait_ge(gate_lo_ready, i * HC + h + 1)
                if h == 0 and first:
                    pe.wait_ge(down_folded, HC)
                elif h == 0:
                    pe.wait_ge(out_ready, i * TILES)
                for t in range(TILES):
                    for n, (g, f) in enumerate(((gate_hi, f2_hi(h)), (gate_hi, f2_lo[0:w, h, :]),
                                                (gate_lo, f2_hi(h)))):
                        mm = pe.matmul(down_bank[t][:, :], g[0:w, h % 2, t * P:(t + 1) * P], f,
                                       start=(h == 0 and n == 0), stop=(h == HC - 1 and n == 2))
                    if h == HC - 1:
                        mm.then_inc(down_filled, 1)

            def block_of_rows(i, first, more):
                pe.wait_ge(c_lo_ready, BT * (i + 1))
                up(i, 0, first)
                for h in range(1, HC - 1):
                    up(i, h, first)
                    down(i, h - 1, first)
                up(i, HC - 1, first)
                if more:
                    convolve(i + 1)
                down(i, HC - 2, first)
                down(i, HC - 1, first)

            pe.wait_ge(near_zeroed, 2)
            pe.wait_ge(down_stacked, 5)
            pe.wait_ge(down_lo_stacked, 2)
            pe.wait_ge(f2_loaded, 16 * len(f2_loads))
            pe.wait_ge(ctx_lo_ready, BLOCKS * PAIRS)
            convolve(0, first=True)
            blocks(pe, block_of_rows)


def layouts(a):
    perm = lambda w: w.reshape(*w.shape[:-1], P, BT).swapaxes(-1, -2).reshape(w.shape)
    wkv = a["L0_attn_Wkv"].reshape(DC, P, G, 2, HD)
    conv = np.zeros((BT, S, NEAR, BT, S), a["L0_cond2_weight"].dtype)
    for m in range(NEAR):
        for r in range(BT):
            for s in range(BT):
                tap = BT * (m - 1) + r - s + TAPS // 2
                if 0 <= tap < TAPS:
                    for co in range(S):
                        first = co // CG * CG
                        conv[r, first:first + CG, m, s, co] = a["L0_cond2_weight"][co, :, tap]
    t = lambda w: w.swapaxes(-1, -2)

    def stacked(factors, rows, width):
        to = np.zeros((3, S, width), factors[0][0].dtype)
        for (w, col), row in zip(factors, rows):
            to[:, row:row + R, col:col + w.shape[1]] = w
        return to.reshape(STACK, width)

    mix_w = a["L0_cond_weight"].reshape(K, S // BT, BT, 1, S).transpose(2, 0, 1, 3, 4)
    mix_wide = np.zeros((BT, S, S // BT, BT, S), mix_w.dtype)
    mix_wide[:, :K] = mix_w
    given = {"cond_t": t(a["cond_128"]), "w0": a["L0_cond_W0"], "w1": a["L0_cond_W1"], "w2": a["L0_cond_W2"],
             "b0": a["L0_cond_b0"].reshape(COND, 1), "b1": a["L0_cond_b1"].reshape(COND, 1),
             "conv_cond": t(a["L0_cond2_c_weight"]), "mix_w": mix_wide.reshape(P, S * S),
             "mix_b": a["L0_cond_bias_k"], "b2": a["L0_cond_b2"].reshape(1, K),
             "conv_bias": a["fside_S_0"].reshape(1, S)}
    params = np.concatenate([np.pad(given[k], ((0, P - given[k].shape[0]), (0, 0))) for k in PARAMS], axis=1)
    return {
        "x": a["x"].reshape(N, D), "params": params,
        "wq": a["L0_attn_Wq"].reshape(DC, P, G, REP, HD).transpose(1, 0, 3, 2, 4).reshape(P, DC, REP, GD),
        "wk": wkv[:, :, :, 0].transpose(1, 0, 2, 3).reshape(P, DC, GD),
        "wv": wkv[:, :, :, 1].transpose(1, 0, 2, 3).reshape(P, DC, GD),
        "wo": perm(a["L0_attn_Wo"].reshape(G, REP, HD, D).transpose(0, 2, 1, 3)).reshape(GD, REP, D),
        "bo": perm(a["L0_attn_bo"].reshape(1, D)),
        "conv": conv.reshape(P, NEAR, P),
        "f1": a["L0_ffn_w1"].reshape(HID, P, BT).transpose(1, 2, 0),
        "f3": a["L0_ffn_w3"].reshape(HID, P, BT).transpose(1, 2, 0),
        "f2": perm(t(a["L0_ffn_w2"])),
        "up_factors": stacked([(perm(a["L0_ffn_lora_A1"]), 0), (perm(a["L0_ffn_lora_A3"]), D),
                               (t(a["L0_ffn_lora_B1"]), 2 * D), (t(a["L0_ffn_lora_B3"]), 2 * D)],
                              (0, R, 0, R), 2 * D + HID),
        "down_factors": stacked([(a["L0_ffn_lora_A2"], 0), (perm(t(a["L0_ffn_lora_B2"])), HID)], (0, 0), HID + D),
        "ident": np.eye(P, dtype=np.float32),
        "causal": np.where(np.arange(S)[None, :] > np.arange(P)[:, None] % S, -1e30, 0.0).astype(np.float32),
    }


def kernel(**inputs):
    import concourse.bacc as bacc
    from concourse.bass_utils import run_bass_kernel_spmd

    nc = bacc.Bacc("TRN2", target_bir_lowering=False, num_devices=1)
    arrays = {f"in_{k}": np.ascontiguousarray(v) for k, v in
              layouts({k: np.asarray(v) for k, v in inputs.items()}).items()}
    args = {k[3:]: nc.dram_tensor(k, v.shape, mybir.dt.from_np(v.dtype), kind="ExternalInput").ap()
            for k, v in arrays.items()}
    out = nc.dram_tensor("out", (N, D), F32, kind="ExternalOutput").ap()
    adaln_attention_ffn(nc, out=out, **args)
    r = run_bass_kernel_spmd(nc, [arrays], core_ids=[0])
    got = r.results[0]["out"]
    return got.reshape(B, S, BT, P).swapaxes(2, 3).reshape(B, S, D)
```
